# Optimizing a Trainium2 kernel written in Bass

```python
import numpy as np
import jax
import jax.numpy as jnp

def _softmax(x, axis=-1):
    return jax.nn.softmax(x, axis=axis)

def _gelu(x):
    return jax.nn.gelu(x, approximate=True)

def _silu(x):
    return jax.nn.silu(x)

def _sigmoid(x):
    return jax.nn.sigmoid(x)

def _layernorm(x, axis=-1, eps=1e-05):
    m = jnp.mean(x, axis=axis, keepdims=True)
    v = jnp.var(x, axis=axis, keepdims=True)
    return (x - m) / jnp.sqrt(v + eps)

def _scatter_add(tgt, idx, src, axis=0):
    return tgt.at[idx].add(src)

def _segment_sum(src, seg, n):
    return jax.ops.segment_sum(src, seg, n)
kernel_name = 'mk_gnn_preln_d4_gnn_r16_561742'

def setup_inputs(seed: int=0):
    np.random.seed(seed)
    _w = jnp.asarray

    def _rec_inputs():
        import jax
        import jax.numpy as jnp
        _gk = jax.random.key(seed)
        x = -0.0003713 + 1 * jax.random.normal(jax.random.fold_in(_gk, 1), (6250, 256), jnp.float32)
        src = jax.random.randint(jax.random.fold_in(_gk, 2), (100000,), 0, 6250, jnp.int32)
        dst = jax.random.randint(jax.random.fold_in(_gk, 3), (100000,), 0, 6250, jnp.int32)
        _o = jnp.argsort(dst, stable=True)
        src = src[_o]
        dst = dst[_o]
        edge_attr_128 = -5.16925e-05 + 1.00005 * jax.random.normal(jax.random.fold_in(_gk, 11), (100000, 128), jnp.float32)
        edge_attr_32 = -5.25733e-05 + 1.00007 * jax.random.normal(jax.random.fold_in(_gk, 12), (100000, 32), jnp.float32)
        edge_weight = jax.random.uniform(jax.random.fold_in(_gk, 14), (100000,), jnp.float32, 0.0, 0.999998)
        return (x, src, dst, edge_attr_128, edge_attr_32, edge_weight)
    x, src, dst, edge_attr_128, edge_attr_32, edge_weight = _rec_inputs()

    def _L0_gnn_setup():
        import jax, jax.numpy as jnp
        import numpy as np
        N_NODES = 3125
        N_EDGES = 50000
        D_MODEL = 256
        NUM_HEADS = 8
        HEAD_DIM = D_MODEL // NUM_HEADS
        D_FF = 2 * D_MODEL
        NEG_SLOPE = 0.2
        BN_EPS = 1e-05

        def _batch_norm(h, g, b):
            mean = jnp.mean(h, axis=0)
            var = jnp.mean((h - mean) ** 2, axis=0)
            return (h - mean) * jax.lax.rsqrt(var + BN_EPS) * g + b
        key = jax.random.key(seed)
        ks = jax.random.split(key, 16)
        x = jax.random.normal(ks[0], (N_NODES, D_MODEL), dtype=jnp.float32)
        src = jax.random.randint(ks[1], (N_EDGES,), 0, N_NODES)
        off = jax.random.randint(ks[2], (N_EDGES,), 1, N_NODES)
        dst = (src + off) % N_NODES
        edge_index = jnp.stack([src, dst]).astype(jnp.int64)

        def lin(k, fi, fo):
            s = 1.0 / np.sqrt(fi)
            return jax.random.uniform(k, (fi, fo), jnp.float32, -s, s)
        inp = {'x': x, 'edge_index': edge_index, 'Wq': lin(ks[3], D_MODEL, D_MODEL), 'bq': jnp.zeros((D_MODEL,), jnp.float32), 'Wk': lin(ks[4], D_MODEL, D_MODEL), 'bk': jnp.zeros((D_MODEL,), jnp.float32), 'Wv': lin(ks[5], D_MODEL, D_MODEL), 'bv': jnp.zeros((D_MODEL,), jnp.float32), 'Wo': lin(ks[6], D_MODEL, D_MODEL), 'bo': jnp.zeros((D_MODEL,), jnp.float32), 'W1': lin(ks[7], D_MODEL, D_FF), 'b1': jnp.zeros((D_FF,), jnp.float32), 'W2': lin(ks[8], D_FF, D_MODEL), 'b2': jnp.zeros((D_MODEL,), jnp.float32), 'bn1_g': jnp.ones((D_MODEL,), jnp.float32), 'bn1_b': jnp.zeros((D_MODEL,), jnp.float32), 'bn2_g': jnp.ones((D_MODEL,), jnp.float32), 'bn2_b': jnp.zeros((D_MODEL,), jnp.float32)}
        return inp
    _L0_gnn_all = _L0_gnn_setup()
    _L0_gnn_in = {k: v for k, v in _L0_gnn_all.items() if k in ('Wq', 'bq', 'Wk', 'bk', 'Wv', 'bv', 'Wo', 'bo', 'W1', 'b1', 'W2', 'b2', 'bn1_g', 'bn1_b', 'bn2_g', 'bn2_b')}
    del _L0_gnn_all

    def _L1_gnn_setup():
        import jax, jax.numpy as jnp
        import numpy as np
        PI = float(np.pi)
        CUTOFF = 5.0
        N_NODES, N_EDGES = (3125, 31250)
        HIDDEN, FILTERS, RADIAL = (256, 128, 32)
        key = jax.random.key(seed)
        ks = jax.random.split(key, 12)
        inv = lambda f: 1.0 / np.sqrt(f)
        return {'x': jax.random.normal(ks[0], (N_NODES, HIDDEN), jnp.float32), 'rbf': jax.random.normal(ks[1], (N_EDGES, RADIAL), jnp.float32), 'dists': jax.random.uniform(ks[2], (N_EDGES,), jnp.float32), 'edge_index': jax.random.randint(ks[3], (2, N_EDGES), 0, N_NODES, jnp.int64), 'W_n2m': jax.random.uniform(ks[4], (FILTERS, HIDDEN), jnp.float32, -inv(HIDDEN), inv(HIDDEN)), 'b_n2m': jnp.zeros((FILTERS,), jnp.float32), 'W_r2m': jax.random.uniform(ks[5], (FILTERS, RADIAL), jnp.float32, -inv(RADIAL), inv(RADIAL)), 'b_r2m': jnp.zeros((FILTERS,), jnp.float32), 'W_lin1': jax.random.uniform(ks[6], (FILTERS, FILTERS), jnp.float32, -inv(FILTERS), inv(FILTERS)), 'W_lin2': jax.random.uniform(ks[7], (FILTERS, FILTERS), jnp.float32, -inv(FILTERS), inv(FILTERS)), 'b_lin2': jnp.zeros((FILTERS,), jnp.float32), 'W_m2n': jax.random.uniform(ks[8], (HIDDEN, FILTERS), jnp.float32, -inv(FILTERS), inv(FILTERS))}
    _L1_gnn_all = _L1_gnn_setup()
    _L1_gnn_in = {k: v for k, v in _L1_gnn_all.items() if k in ('W_n2m', 'b_n2m', 'W_r2m', 'b_r2m', 'W_lin1', 'W_lin2', 'b_lin2', 'W_m2n')}
    del _L1_gnn_all

    def _L2_gnn_setup():
        import jax, jax.numpy as jnp
        import numpy as np
        N_NODES = 3125
        N_EDGES = 50000
        IN_DIM = 256
        OUT_DIM = 256
        HEADS = 1
        EDGE_DIM = 128
        NEG_SLOPE = 0.01
        key = jax.random.key(seed)
        ks = jax.random.split(key, 8)
        x = jax.random.normal(ks[0], (N_NODES, IN_DIM), dtype=jnp.float32)
        edge_index = jax.random.randint(ks[1], (2, N_EDGES), 0, N_NODES, dtype=jnp.int64)
        edge_attr = jax.random.normal(ks[2], (N_EDGES, EDGE_DIM), dtype=jnp.float32)
        hc = HEADS * OUT_DIM
        Wn = jax.random.normal(ks[3], (hc, IN_DIM), dtype=jnp.float32) / np.sqrt(IN_DIM)
        bn = jnp.zeros((hc,), dtype=jnp.float32)
        We = jax.random.normal(ks[4], (hc, EDGE_DIM), dtype=jnp.float32) / np.sqrt(EDGE_DIM)
        be = jnp.zeros((hc,), dtype=jnp.float32)
        attn = jax.random.normal(ks[5], (1, HEADS, OUT_DIM), dtype=jnp.float32) * np.sqrt(2.0 / (HEADS * OUT_DIM + 1))
        return {'x': x, 'edge_index': edge_index, 'edge_attr': edge_attr, 'Wn': Wn, 'bn': bn, 'We': We, 'be': be, 'attn': attn}
    _L2_gnn_all = _L2_gnn_setup()
    _L2_gnn_in = {k: v for k, v in _L2_gnn_all.items() if k in ('Wn', 'bn', 'We', 'be', 'attn')}
    del _L2_gnn_all

    def _L3_gnn_setup():
        import jax, jax.numpy as jnp
        import numpy as np
        N_NODES = 3125
        N_EDGES = 50000
        D_IN = 256
        D_OUT = 256
        key = jax.random.key(seed)
        k1, k2, k3 = jax.random.split(key, 3)
        x = jax.random.normal(k1, (N_NODES, D_IN), dtype=jnp.float32)
        edge_index = jax.random.randint(k2, (2, N_EDGES), 0, N_NODES, dtype=jnp.int64)
        W = jax.random.normal(k3, (D_IN, D_OUT), dtype=jnp.float32) * (1.0 / np.sqrt(D_IN))
        b = jnp.zeros((D_OUT,), dtype=jnp.float32)
        return {'x': x, 'edge_index': edge_index, 'W': W, 'b': b}
    _L3_gnn_all = _L3_gnn_setup()
    _L3_gnn_in = {k: v for k, v in _L3_gnn_all.items() if k in ('W', 'b')}
    del _L3_gnn_all
    return {'x': x, 'src': src, 'dst': dst, 'edge_attr_128': edge_attr_128, 'edge_attr_32': edge_attr_32, 'edge_weight': edge_weight, 'L0_gnn_Wq': _L0_gnn_in['Wq'], 'L0_gnn_bq': _L0_gnn_in['bq'], 'L0_gnn_Wk': _L0_gnn_in['Wk'], 'L0_gnn_bk': _L0_gnn_in['bk'], 'L0_gnn_Wv': _L0_gnn_in['Wv'], 'L0_gnn_bv': _L0_gnn_in['bv'], 'L0_gnn_Wo': _L0_gnn_in['Wo'], 'L0_gnn_bo': _L0_gnn_in['bo'], 'L0_gnn_W1': _L0_gnn_in['W1'], 'L0_gnn_b1': _L0_gnn_in['b1'], 'L0_gnn_W2': _L0_gnn_in['W2'], 'L0_gnn_b2': _L0_gnn_in['b2'], 'L0_gnn_bn1_g': _L0_gnn_in['bn1_g'], 'L0_gnn_bn1_b': _L0_gnn_in['bn1_b'], 'L0_gnn_bn2_g': _L0_gnn_in['bn2_g'], 'L0_gnn_bn2_b': _L0_gnn_in['bn2_b'], 'L1_gnn_W_n2m': _L1_gnn_in['W_n2m'], 'L1_gnn_b_n2m': _L1_gnn_in['b_n2m'], 'L1_gnn_W_r2m': _L1_gnn_in['W_r2m'], 'L1_gnn_b_r2m': _L1_gnn_in['b_r2m'], 'L1_gnn_W_lin1': _L1_gnn_in['W_lin1'], 'L1_gnn_W_lin2': _L1_gnn_in['W_lin2'], 'L1_gnn_b_lin2': _L1_gnn_in['b_lin2'], 'L1_gnn_W_m2n': _L1_gnn_in['W_m2n'], 'L2_gnn_Wn': _L2_gnn_in['Wn'], 'L2_gnn_bn': _L2_gnn_in['bn'], 'L2_gnn_We': _L2_gnn_in['We'], 'L2_gnn_be': _L2_gnn_in['be'], 'L2_gnn_attn': _L2_gnn_in['attn'], 'L3_gnn_W': _L3_gnn_in['W'], 'L3_gnn_b': _L3_gnn_in['b']}

def reference(x, src, dst, edge_attr_128, edge_attr_32, edge_weight, L0_gnn_Wq, L0_gnn_bq, L0_gnn_Wk, L0_gnn_bk, L0_gnn_Wv, L0_gnn_bv, L0_gnn_Wo, L0_gnn_bo, L0_gnn_W1, L0_gnn_b1, L0_gnn_W2, L0_gnn_b2, L0_gnn_bn1_g, L0_gnn_bn1_b, L0_gnn_bn2_g, L0_gnn_bn2_b, L1_gnn_W_n2m, L1_gnn_b_n2m, L1_gnn_W_r2m, L1_gnn_b_r2m, L1_gnn_W_lin1, L1_gnn_W_lin2, L1_gnn_b_lin2, L1_gnn_W_m2n, L2_gnn_Wn, L2_gnn_bn, L2_gnn_We, L2_gnn_be, L2_gnn_attn, L3_gnn_W, L3_gnn_b):
    import jax
    import jax.numpy as jnp

    def _L0_gnn_ref(x, edge_index, Wq, bq, Wk, bk, Wv, bv, Wo, bo, W1, b1, W2, b2, bn1_g, bn1_b, bn2_g, bn2_b):
        import jax, jax.numpy as jnp
        import numpy as np
        N_NODES = 3125
        N_EDGES = 50000
        D_MODEL = 256
        NUM_HEADS = 8
        HEAD_DIM = D_MODEL // NUM_HEADS
        D_FF = 2 * D_MODEL
        NEG_SLOPE = 0.2
        BN_EPS = 1e-05

        def _batch_norm(h, g, b):
            mean = jnp.mean(h, axis=0)
            var = jnp.mean((h - mean) ** 2, axis=0)
            return (h - mean) * jax.lax.rsqrt(var + BN_EPS) * g + b
        N = x.shape[0]
        Qh = (x @ Wq + bq).reshape(N, NUM_HEADS, HEAD_DIM)
        Kh = (x @ Wk + bk).reshape(N, NUM_HEADS, HEAD_DIM)
        Vh = (x @ Wv + bv).reshape(N, NUM_HEADS, HEAD_DIM)
        s = jnp.einsum('nhc,nhc->nh', Qh, Kh) / jnp.sqrt(jnp.float32(HEAD_DIM))
        loops = jnp.arange(N, dtype=edge_index.dtype)
        src = jnp.concatenate([edge_index[0], loops])
        dst = jnp.concatenate([edge_index[1], loops])
        alpha = jax.nn.leaky_relu(s[src] + s[dst], NEG_SLOPE)
        m = jax.ops.segment_max(alpha, dst, num_segments=N)
        e = jnp.exp(alpha - m[dst])
        denom = jax.ops.segment_sum(e, dst, num_segments=N)
        a = e / denom[dst]
        msg = Vh[src] * a[:, :, None]
        attn = jax.ops.segment_sum(msg, dst, num_segments=N).reshape(N, D_MODEL)
        h = attn @ Wo + bo
        h = x + h
        h = _batch_norm(h, bn1_g, bn1_b)
        h2 = jax.nn.relu(h @ W1 + b1) @ W2 + b2
        h = _batch_norm(h + h2, bn2_g, bn2_b)
        return h

    def _L1_gnn_ref(x, rbf, dists, edge_index, W_n2m, b_n2m, W_r2m, b_r2m, W_lin1, W_lin2, b_lin2, W_m2n):
        import jax, jax.numpy as jnp
        import numpy as np
        PI = float(np.pi)
        CUTOFF = 5.0
        N_NODES, N_EDGES = (3125, 31250)
        HIDDEN, FILTERS, RADIAL = (256, 128, 32)
        edge_attr = rbf @ W_r2m.T + b_r2m
        h = x @ W_n2m.T + b_n2m
        C = 0.5 * (jnp.cos(dists * (PI / CUTOFF)) + 1.0)
        W = edge_attr * C[:, None]
        h = h @ W_lin1.T
        msg = h[edge_index[0]] * W
        agg = jax.ops.segment_sum(msg, edge_index[1], num_segments=x.shape[0])
        h = agg @ W_lin2.T + b_lin2
        return h @ W_m2n.T

    def _L2_gnn_ref(x, edge_index, edge_attr, Wn, bn, We, be, attn):
        import jax, jax.numpy as jnp
        import numpy as np
        N_NODES = 3125
        N_EDGES = 50000
        IN_DIM = 256
        OUT_DIM = 256
        HEADS = 1
        EDGE_DIM = 128
        NEG_SLOPE = 0.01
        N = x.shape[0]
        H, C = (attn.shape[1], attn.shape[2])
        src, dst = (edge_index[0], edge_index[1])
        h = x @ Wn.T + bn
        e = edge_attr @ We.T + be
        xj = h[src].reshape(-1, H, C)
        ee = e.reshape(-1, H, C)
        a = jax.nn.leaky_relu(jnp.sum((xj + ee) * attn, axis=-1), NEG_SLOPE)
        m = jax.ops.segment_max(a, dst, num_segments=N)
        a = jnp.exp(a - m[dst])
        denom = jax.ops.segment_sum(a, dst, num_segments=N)
        a = a / (denom[dst] + 1e-16)
        msg = (xj * a[..., None]).reshape(-1, H * C)
        out = jax.ops.segment_sum(msg, dst, num_segments=N)
        return jax.nn.relu(out)

    def _L3_gnn_ref(x, edge_index, W, b):
        import jax, jax.numpy as jnp
        import numpy as np
        N_NODES = 3125
        N_EDGES = 50000
        D_IN = 256
        D_OUT = 256
        N = x.shape[0]
        loops = jnp.arange(N, dtype=edge_index.dtype)
        src = jnp.concatenate([edge_index[0], loops])
        dst = jnp.concatenate([edge_index[1], loops])
        deg = jax.ops.segment_sum(jnp.ones_like(dst, dtype=x.dtype), dst, num_segments=N)
        dinv = jax.lax.rsqrt(deg)
        norm = dinv[src] * dinv[dst]
        xw = jnp.matmul(x, W)
        msg = xw[src] * norm[:, None]
        agg = jax.ops.segment_sum(msg, dst, num_segments=N)
        return jax.nn.relu(agg + b)
    edge_index = jnp.stack([src, dst])
    h = jnp.maximum(_layernorm(x, axis=-1), 0.0)
    x = x + _L0_gnn_ref(h, edge_index, L0_gnn_Wq, L0_gnn_bq, L0_gnn_Wk, L0_gnn_bk, L0_gnn_Wv, L0_gnn_bv, L0_gnn_Wo, L0_gnn_bo, L0_gnn_W1, L0_gnn_b1, L0_gnn_W2, L0_gnn_b2, L0_gnn_bn1_g, L0_gnn_bn1_b, L0_gnn_bn2_g, L0_gnn_bn2_b)
    h = jnp.maximum(_layernorm(x, axis=-1), 0.0)
    x = x + _L1_gnn_ref(h, edge_attr_32, edge_weight, edge_index, L1_gnn_W_n2m, L1_gnn_b_n2m, L1_gnn_W_r2m, L1_gnn_b_r2m, L1_gnn_W_lin1, L1_gnn_W_lin2, L1_gnn_b_lin2, L1_gnn_W_m2n)
    h = jnp.maximum(_layernorm(x, axis=-1), 0.0)
    x = x + _L2_gnn_ref(h, edge_index, edge_attr_128, L2_gnn_Wn, L2_gnn_bn, L2_gnn_We, L2_gnn_be, L2_gnn_attn)
    h = jnp.maximum(_layernorm(x, axis=-1), 0.0)
    x = x + _L3_gnn_ref(h, edge_index, L3_gnn_W, L3_gnn_b)
    return x

_drawn_inputs = setup_inputs


def setup_inputs(seed=0):
    import zlib

    import numpy as np

    out = dict(_drawn_inputs(seed))
    spreads = {'L0_gnn_bq': (0.0, 0.8),
     'L0_gnn_bk': (0.0, 0.8),
     'L0_gnn_bv': (0.0, 2.0),
     'L0_gnn_bo': (0.0, 2.0),
     'L0_gnn_b1': (0.0, 0.538),
     'L0_gnn_b2': (0.0, 2.0),
     'L0_gnn_bn1_g': (1.0, 0.538),
     'L0_gnn_bn1_b': (0.0, 0.8),
     'L0_gnn_bn2_g': (1.0, 0.2),
     'L0_gnn_bn2_b': (0.0, 0.1),
     'L1_gnn_b_n2m': (0.0, 0.302),
     'L1_gnn_b_r2m': (0.0, 0.31),
     'L1_gnn_b_lin2': (0.0, 0.273),
     'L2_gnn_bn': (0.0, 0.1),
     'L2_gnn_be': (0.0, 2.0),
     'L3_gnn_b': (0.0, 0.1)}
    factors = {'edge_weight': 8.0, 'L0_gnn_Wq': 8.0, 'L0_gnn_Wk': 8.0}
    for name, (base, spread) in spreads.items():
        noise = np.random.default_rng([zlib.crc32(name.encode()), seed]).standard_normal(out[name].shape)
        drawn = base * np.exp(spread * noise) if base else spread * noise
        out[name] = jnp.asarray(drawn.astype(out[name].dtype))
    for name, factor in factors.items():
        out[name] = (out[name] * factor).astype(out[name].dtype)
    return out
```

```python
from contextlib import ExitStack

import numpy as np

import concourse.bass as bass
from concourse import mybir

F32 = mybir.dt.float32
BF16 = mybir.dt.bfloat16
I32 = mybir.dt.int32
ALU = mybir.AluOpType
ACT = mybir.ActivationFunctionType
AX_X = mybir.AxisListType.X
DVE_ENGINE = mybir.EngineType.DVE
PE_ENGINE = mybir.EngineType.PE
SP_ENGINE = mybir.EngineType.SP

P = 128
N_NODES, N_EDGES = 6250, 100000
D = 256
HEADS, HEAD_DIM = 8, 32
FF = 512
FILTERS, RADIAL = 128, 32
EDGE_DIM = 128
NB = -(-N_NODES // P)
N_PAD = NB * P
LAST = N_NODES - (NB - 1) * P
TILES = -(-N_EDGES // P)
GROUPS = -(-TILES // P)
E_PAD = GROUPS * P * P
G = 8
RING = 4
BATCHES = -(-(TILES + NB - 1) // G)
TURNS = BATCHES // RING
STEPS = (BATCHES + 3) * G
HALF = STEPS // 2
SLOTS = G * P
NO_NODE = 1 << 24
BIG = 1e30
LN_EPS = BN_EPS = 1e-5
ATT0_SLOPE, ATT2_SLOPE = 0.2, 0.01
CUTOFF = 5.0
ROUNDER = 1.5 * 2.0 ** 23
ROW0 = D + HEADS
ACC_W = D + 2 * HEADS + 1
ROW2 = D + 2
CHUNK = 448
CHUNKS = N_PAD // CHUNK
BN_CHUNK = 250
BN_CHUNKS = N_NODES // BN_CHUNK

CONST = {}
_at = 0
for _name, _w in (("iota_k", STEPS), ("iota_n", P), ("ident", P), ("tile", GROUPS), ("p_first", 1), ("p_last", 1)):
    CONST[_name] = (_at, _at + _w)
    _at += _w
CONST_W = _at

COLS = {}
_at = 0
for _name, _w in (("bo", 2), ("bn1_g", 2), ("bn1_b", 2), ("b1", 4), ("b2", 2), ("bn2_g", 2), ("bn2_b", 2),
                  ("b_n2m", 1), ("b_lin2", 1), ("be", 2), ("attn", 2)):
    COLS[_name] = (_at, _at + _w)
    _at += _w
COLS_W = _at


def ready(b):
    return b + 3


def free(b):
    return b + 1


def each_pair(eng, count, body, peeled=0):
    for b in range(peeled):
        body(b, b % 2, True)
    with eng.Fori(peeled // 2, (count - 1) // 2) as i:
        body(2 * i, 0, True)
        body(2 * i + 1, 1, True)
    if count % 2 == 0:
        body(count - 2, 0, True)
    body(count - 1, (count - 1) % 2, False)


def build(nc, inp, out):
    top = ExitStack()
    with top:
        carriers = nc.alloc_semaphore("carriers")
        held = []

        def sem(name):
            held.append(nc.alloc_semaphore(name))
            return held[-1]

        def layer_ends():
            nc.clear_and_free_semaphores(held)
            held.clear()
            nc.all_engine_barrier()

        def sb(stack, name, shape, dt=F32):
            return stack.enter_context(nc.sbuf_tensor(name, shape, dt))

        def scratch(name, shape, dt=F32):
            return nc.dram_tensor(name, shape, dt, kind="Internal").ap()

        table0 = scratch("table0", (N_PAD, ROW0))
        table1 = scratch("table1", (N_PAD, FILTERS))
        table2 = scratch("table2", (N_PAD, ROW2))
        table3 = scratch("table3", (N_PAD, D))
        key_line = scratch("key_line", (1 + GROUPS * P * P,))
        restart_line = scratch("restart_line", (GROUPS * P * P + 1,), BF16)

        banks = top.enter_context(nc.psum_tensor("banks", [P, 8, 512], F32))

        const = sb(top, "const", [P, CONST_W])
        cols = sb(top, "cols", [P, COLS_W])
        X = sb(top, "X", [P, NB, D])
        acc = sb(top, "acc", [P, NB, ACC_W])
        src_idx = sb(top, "src_idx", [P, STEPS], I32)
        dst_loc = sb(top, "dst_loc", [P, STEPS])
        cutoff = sb(top, "cutoff", [P, STEPS])
        edge_q = sb(top, "edge_q", [P, STEPS])
        step_block = sb(top, "step_block", [1, STEPS], I32)
        step_tile = sb(top, "step_tile", [1, STEPS], I32)
        same_first = sb(top, "same_first", [P, BATCHES + 1])
        same_last = sb(top, "same_last", [P, BATCHES + 1])
        stats = sb(top, "stats", [P, NB, 6])
        rstd = sb(top, "rstd", [P, NB])
        nbias = sb(top, "nbias", [P, NB])
        degree = sb(top, "degree", [P, NB])
        dinv = sb(top, "dinv", [P, NB])
        eps = sb(top, "eps", [P, 1])
        ones = sb(top, "ones", [P, P])
        scores = sb(top, "scores", [P, NB, HEADS])

        def const_(name):
            return const[:, CONST[name][0]:CONST[name][1]]

        def col(name, f=0):
            return cols[:, COLS[name][0] + f:COLS[name][0] + f + 1]

        ident = const_("ident")
        iota_n = const_("iota_n")

        def node_rows(ap, b):
            return ap[bass.ds(b * P, P), :]

        st = ExitStack()
        with st:
            dst_i = sb(st, "dst_i", [P, GROUPS, P], I32)
            src_i = sb(st, "src_i", [P, GROUPS, P], I32)
            next_i = sb(st, "next_i", [P, GROUPS, 1], I32)
            block_i = sb(st, "block_i", [P, 2, GROUPS], I32)
            dst_f = sb(st, "dst_f", [P, GROUPS, P])
            src_f = sb(st, "src_f", [P, GROUPS, P])
            wgt = sb(st, "wgt", [P, GROUPS, P])
            turn = sb(st, "turn", [P, GROUPS, P])
            first_step = sb(st, "first_step", [P, 2, GROUPS])
            work = acc[:, :, :].rearrange("p b w -> p (b w)")[:, 0:2 * GROUPS * STEPS].rearrange("p (o g k) -> p o g k", o=2, g=GROUPS)
            begun, pick = work[:, 0, :, :], work[:, 1, :, :]
            block = sb(st, "block", [P, STEPS])
            valid = sb(st, "valid", [P, 2, STEPS])
            key = sb(st, "key", [P, GROUPS * P])
            key_row = sb(st, "key_row", [P, GROUPS, P])
            key_prev = sb(st, "key_prev", [P, GROUPS, P])
            differ = sb(st, "differ", [P, GROUPS, P])
            restart = sb(st, "restart", [P, GROUPS, P], BF16)
            mark = sb(st, "mark", [1, 1])
            mark_b = sb(st, "mark_b", [1, 1], BF16)
            goes_on_b = sb(st, "goes_on_b", [1, BATCHES + 1], BF16)
            goes_on = sb(st, "goes_on", [1, BATCHES + 1])

            const_in, dst_in, src_in, next_in, wgt_in, x_in = (sem(n) for n in (
                "const_in", "dst_in", "src_in", "next_in", "wgt_in", "x_in"))
            idx_dve = sem("idx_dve")
            sine_done = sem("sine_done")
            picked = sem("picked")
            key_turned = sem("key_turned")
            key_rows = sem("key_rows")
            key_out, key_back, restart_out, goes_on_in = (sem(n) for n in (
                "key_out", "key_back", "restart_out", "goes_on_in"))
            goes_on_ready, goes_on_spread = sem("goes_on_ready"), sem("goes_on_spread")
            restart_ready = sem("restart_ready")

            with nc.Block() as blk:
                at = {}

                @blk.vector
                def _(dve):
                    def step(ins, name=""):
                        at["last"] = at.get("last", 0) + 1
                        at[name] = at["last"]
                        ins.then_inc(idx_dve, 1)
                        return at["last"]

                    v = nc.vector
                    v.memset(eps[:, :], LN_EPS)
                    v.memset(ones[:, :], 1.0)
                    v.memset(mark[:, :], -1.0)
                    v.memset(mark_b[:, :], -BIG)
                    step(v.memset(key[:, :], 0.0))
                    dve.wait_ge(dst_in, 16)
                    dve.wait_ge(next_in, 16)
                    v.tensor_scalar(block_i[:, 0, :].unsqueeze(2), dst_i[:, :, 0:1], 7, None, ALU.arith_shift_right)
                    v.tensor_scalar(block_i[:, 1, :].unsqueeze(2), next_i[:, :, :], 7, None, ALU.arith_shift_right)
                    dve.wait_ge(const_in, 32)
                    now = step(v.tensor_copy(dst_f[:, :, :], dst_i[:, :, :]))
                    dve.wait_ge(idx_dve, now)
                    v.tensor_tensor(first_step[:, 0, :], block_i[:, 0, :], const_("tile"), ALU.add)
                    now = step(v.scalar_tensor_tensor(first_step[:, 1, :], block_i[:, 1, :], 1.0, const_("tile"), ALU.add, ALU.add))
                    dve.wait_ge(src_in, 16)
                    now = step(v.tensor_copy(src_f[:, :, :], src_i[:, :, :]))
                    dve.wait_ge(idx_dve, now)
                    for g in range(GROUPS):
                        last = v.tensor_scalar(begun[:, g, :], const_("iota_k"), first_step[:, 0, g:g + 1], None, ALU.is_ge)
                    now = step(last)
                    dve.wait_ge(idx_dve, now)
                    for g in range(GROUPS):
                        last = v.scalar_tensor_tensor(pick[:, g, :], const_("iota_k"), first_step[:, 1, g:g + 1], begun[:, g, :], ALU.is_lt, ALU.mult)
                    dve.wait_ge(wgt_in, 16)
                    now = step(v.tensor_scalar(turn[:, :, :], wgt[:, :, :], 0.5 / CUTOFF, None, ALU.mult), "pick")
                    dve.wait_ge(idx_dve, now)
                    now = step(v.tensor_scalar(wgt[:, :, :], turn[:, :, :], ROUNDER, None, ALU.add))
                    dve.wait_ge(idx_dve, now)
                    now = step(v.tensor_scalar(wgt[:, :, :], wgt[:, :, :], ROUNDER, None, ALU.subtract))
                    dve.wait_ge(idx_dve, now)
                    step(v.tensor_tensor(turn[:, :, :], turn[:, :, :], wgt[:, :, :], ALU.subtract), "turn")
                    dve.wait_ge(sine_done, 1)
                    now = step(v.tensor_tensor(turn[:, :, :], wgt[:, :, :], wgt[:, :, :], ALU.mult))
                    dve.wait_ge(idx_dve, now)
                    step(v.tensor_scalar(turn[:, :, :], turn[:, :, :], -1.0, 1.0, ALU.mult, ALU.add), "cutoff")
                    def halves(tile):
                        return tile[:, :].rearrange("p (h k) -> p h k", h=2)

                    dve.wait_ge(picked, 1)
                    iota_k2 = const_("iota_k").rearrange("p (h k) -> p h k", h=2)
                    now = step(v.scalar_tensor_tensor(halves(block), iota_k2, 1.0, banks[:, 0:2, 0:HALF], ALU.add, ALU.subtract))
                    v.tensor_scalar(step_tile[:, :].rearrange("p (h k) -> p h k", h=2), banks[0:1, 0:2, 0:HALF], 1.0, 0.0, ALU.subtract, ALU.max)
                    dve.wait_ge(idx_dve, now)
                    v.tensor_scalar(step_block[:, :], block[0:1, :], float(NB - 1), None, ALU.min)
                    dve.wait_ge(picked, 2)
                    now = step(v.scalar_tensor_tensor(halves(dst_loc), halves(block), -float(P), banks[:, 2:4, 0:HALF], ALU.mult, ALU.add))
                    dve.wait_ge(picked, 3)
                    v.tensor_copy(halves(src_idx), banks[:, 4:6, 0:HALF])
                    dve.wait_ge(idx_dve, now)
                    now = step(v.tensor_scalar(valid[:, 0, :], dst_loc[:, :], 0.0, None, ALU.is_ge))
                    dve.wait_ge(idx_dve, now)
                    now = step(v.scalar_tensor_tensor(valid[:, 1, :], dst_loc[:, :], float(P), valid[:, 0, :], ALU.is_lt, ALU.mult))
                    dve.wait_ge(idx_dve, now)
                    now = step(v.scalar_tensor_tensor(halves(key[:, 0:STEPS]), banks[:, 2:4, 0:HALF], 1.0, halves(valid[:, 1, :]), ALU.add, ALU.mult))
                    dve.wait_ge(picked, 4)
                    step(v.tensor_copy(halves(cutoff), banks[:, 6:8, 0:HALF]), "key")
                    dve.wait_ge(key_turned, 1)
                    v.tensor_copy(key_row[:, 0:4, :], banks[:, 0, :].rearrange("p (g e) -> p g e", g=4)).then_inc(key_rows, 1)
                    v.tensor_copy(key_row[:, 4:GROUPS, :], banks[:, 1, 0:(GROUPS - 4) * P].rearrange("p (g e) -> p g e", g=GROUPS - 4)).then_inc(key_rows, 1)
                    dve.wait_ge(key_rows, 2)
                    dve.wait_ge(key_back, 16)
                    now = step(v.tensor_tensor(differ[:, :, :], key_row[:, :, :], key_prev[:, :, :], ALU.not_equal))
                    dve.wait_ge(idx_dve, now)
                    v.tensor_scalar(restart[:, :, :], differ[:, :, :], -BIG, None, ALU.mult).then_inc(restart_ready, 1)
                    dve.wait_ge(goes_on_in, 16)
                    v.tensor_scalar(goes_on[:, :], goes_on_b[:, :], 0.0, None, ALU.is_equal).then_inc(goes_on_ready, 1)
                    dve.wait_ge(goes_on_spread, 1)
                    v.tensor_scalar(same_first[:, :], banks[:, 2, 0:BATCHES + 1], const_("p_first"), None, ALU.mult)
                    v.tensor_scalar(same_last[:, :], banks[:, 2, 0:BATCHES + 1], const_("p_last"), None, ALU.mult)
                    dve.wait_ge(x_in, 16)
                    with dve.Fori(0, NB) as b:
                        v.bn_stats(stats[:, bass.ds(b, 1), :].squeeze(1), X[:, bass.ds(b, 1), :].squeeze(1))

                @blk.sync
                def _(sp):
                    sp.dma_start(const[:, :], inp["const"]).then_inc(const_in, 16)
                    sp.dma_start(dst_i[:, :, :], inp["dst"][0:E_PAD].rearrange("(g p e) -> p g e", p=P, e=P)).then_inc(dst_in, 16)
                    with nc.allow_non_contiguous_dma(reason="one word of each tile"):
                        sp.dma_start(next_i[:, :, :], inp["dst"][P:P + E_PAD].rearrange("(g p e) -> p g e", p=P, e=P)[:, :, 0:1]).then_inc(next_in, 16)
                    sp.dma_start(src_i[:, :, :], inp["src"].rearrange("(g p e) -> p g e", p=P, e=P)).then_inc(src_in, 16)
                    sp.dma_start(wgt[:, :, :], inp["edge_weight"].rearrange("(g p e) -> p g e", p=P, e=P)).then_inc(wgt_in, 16)
                    sp.dma_start(cols[:, :], inp["cols"]).then_inc(const_in, 16)
                    sp.dma_start(X[:, :, :], inp["x"].rearrange("(b p) d -> p b d", p=P)).then_inc(x_in, 16)
                    sp.wait_ge(key_rows, 2)
                    sp.dma_start(key_line[1:1 + GROUPS * P * P].rearrange("(g p e) -> p g e", p=P, e=P), key_row[:, :, :]).then_inc(key_out, 16)
                    sp.dma_start(key_line[0:1].unsqueeze(0), mark[:, :]).then_inc(key_out, 16)
                    sp.wait_ge(key_out, 32)
                    sp.dma_start(key_prev[:, :, :], key_line[0:GROUPS * P * P].rearrange("(g p e) -> p g e", p=P, e=P)).then_inc(key_back, 16)
                    sp.wait_ge(restart_ready, 1)
                    sp.dma_start(restart_line[0:GROUPS * P * P].rearrange("(g p e) -> p g e", p=P, e=P), restart[:, :, :]).then_inc(restart_out, 16)
                    sp.dma_start(restart_line[GROUPS * P * P:].unsqueeze(0), mark_b[:, :]).then_inc(restart_out, 16)
                    sp.wait_ge(restart_out, 32)
                    with nc.allow_non_contiguous_dma(reason="one word of each batch"):
                        sp.dma_start(goes_on_b[:, :].unsqueeze(2), restart_line[0:(BATCHES + 1) * SLOTS].rearrange("(o j e) -> o j e", o=1, e=SLOTS)[:, :, 0:1]).then_inc(goes_on_in, 16)
                    sp.wait_ge(x_in, 16)

                @blk.scalar
                def _(act):
                    act.wait_ge(idx_dve, at["turn"])
                    nc.scalar.activation(wgt[:, :, :], turn[:, :, :], ACT.Sin, scale=float(np.pi)).then_inc(sine_done, 1)

                @blk.tensor
                def _(pe):
                    def pick_rows(bank, rows, by):
                        for h in range(2):
                            for g in range(GROUPS):
                                last = nc.tensor.matmul(banks[:, bank + h, 0:HALF], rows(g), by[:, g, h * HALF:(h + 1) * HALF],
                                                        start=(g == 0), stop=(g == GROUPS - 1))
                        last.then_inc(picked, 1)

                    pe.wait_ge(idx_dve, at["pick"])
                    pick_rows(0, lambda g: ones[:, :], begun)
                    pick_rows(2, lambda g: dst_f[:, g, :], pick)
                    pick_rows(4, lambda g: src_f[:, g, :], pick)
                    pe.wait_ge(idx_dve, at["cutoff"])
                    pick_rows(6, lambda g: turn[:, g, :], pick)
                    pe.wait_ge(idx_dve, at["key"])
                    for g in range(GROUPS):
                        last = nc.tensor.transpose(banks[:, g // 4, (g % 4) * P:(g % 4 + 1) * P], key[:, g * P:(g + 1) * P], ident)
                    last.then_inc(key_turned, 1)
                    pe.wait_ge(goes_on_ready, 1)
                    nc.tensor.matmul(banks[:, 2, 0:BATCHES + 1], ones[0:1, :], goes_on[:, :], start=True, stop=True).then_inc(goes_on_spread, 1)

        def norm_coefs(dve, name, work, root_ready, steps):
            v = nc.vector
            mean, diff, var = work[:, 0, :], work[:, 1, :], work[:, 2, :]
            even_mean, even_m2, odd_mean, odd_m2 = (stats[:, :, i] for i in (1, 2, 4, 5))
            n = 0

            def link(ins):
                nonlocal n
                n += 1
                ins.then_inc(steps, 1)
                dve.wait_ge(steps, n)

            v.tensor_tensor(mean, even_mean, odd_mean, ALU.add)
            v.tensor_tensor(diff, even_mean, odd_mean, ALU.subtract)
            link(v.tensor_tensor(var, even_m2, odd_m2, ALU.add))
            v.tensor_scalar(mean, mean, 0.5, None, ALU.mult)
            link(v.scalar_tensor_tensor(diff, diff, 0.25, diff, ALU.mult, ALU.mult))
            link(v.scalar_tensor_tensor(var, var, 1.0 / D, diff, ALU.mult, ALU.add))
            dve.wait_ge(root_ready, 1)
            link(v.reciprocal(rstd[:, :], work[:, 3, :]))
            link(v.scalar_tensor_tensor(nbias[:, :], mean, -1.0, rstd[:, :], ALU.mult, ALU.mult))

        VAR_STEP, COEF_STEP = 3, 5

        def node_stage(tag, weights, weight_cols, load_extra, pe_mm, dve_row, act_mid, pool_extra, table, row_w, row_init, extra_alloc):
            st = ExitStack()
            with st:
                w = sb(st, f"{tag}_w", [P, weight_cols])
                work = sb(st, f"{tag}_work", [P, 4, NB])
                h = sb(st, f"{tag}_h", [P, 2, D])
                hT = sb(st, f"{tag}_hT", [P, 2, 2, P])
                row = sb(st, f"{tag}_row", [P, 2, row_w])
                extra = extra_alloc(st) if extra_alloc else None
                w_in, extra_in = sem(f"{tag}_w_in"), sem(f"{tag}_extra_in") if load_extra else None
                steps, root_ready = sem(f"{tag}_coef_steps"), sem(f"{tag}_root")
                h_ready, turned, hT_ready, product, row_ready = (sem(f"{tag}_{n}") for n in (
                    "h_ready", "turned", "hT_ready", "product", "row_ready"))
                mid_product, mid_ready = (sem(f"{tag}_mid_product"), sem(f"{tag}_mid_ready")) if act_mid else (None, None)
                row_taken = sem(f"{tag}_row_taken") if pool_extra else None
                row_free = [sem(f"{tag}_stored{u}") for u in range(2)]
                chain = sem(f"{tag}_chain") if load_extra else None
                S = dict(w=w, h=h, hT=hT, row=row, extra=extra, product=product, row_ready=row_ready, chain=chain, mid_product=mid_product,
                         mid_ready=mid_ready, hT_ready=hT_ready, row_taken=row_taken)

                with nc.Block() as blk:
                    @blk.sync
                    def _(sp):
                        sp.dma_start(w[:, :], weights).then_inc(w_in, 16)
                        if load_extra:
                            load_extra(sp, extra, extra_in)

                        def store(b, u, _):
                            sp.wait_ge(row_ready, ready(b))
                            sp.sem_inc(carriers, 1)
                            sp.dma_start(node_rows(table, b), row[:, u, :]).then_inc(row_free[u], 16)

                        each_pair(sp, NB, store)
                        for u in range(2):
                            sp.wait_ge(row_free[u], 16 * ((NB + 1 - u) // 2))

                    @blk.gpsimd
                    def _(pool):
                        if tag != "n3":
                            nc.gpsimd.memset(acc[:, :, :], 0.0)
                        if pool_extra:
                            pool.sem_inc(row_taken, 2)
                            each_pair(pool, NB, lambda b, u, _: pool_extra(pool, b, u, S))

                    @blk.scalar
                    def _(act):
                        act.sem_inc(h_ready, 2)
                        act.sem_inc(hT_ready, 2)
                        if act_mid:
                            act.sem_inc(mid_ready, 2)
                        act.wait_ge(steps, VAR_STEP)
                        nc.scalar.activation(work[:, 3, :], work[:, 2, :], ACT.Sqrt, bias=eps[:, 0:1]).then_inc(root_ready, 1)
                        act.wait_ge(steps, COEF_STEP)

                        def normed(b, u):
                            act.wait_ge(turned, free(b))
                            nc.scalar.activation(h[:, u, :], X[:, bass.ds(b, 1), :].squeeze(1), ACT.Relu,
                                                 bias=nbias[:, bass.ds(b, 1)], scale=rstd[:, bass.ds(b, 1)]).then_inc(h_ready, 1)

                        def block(b, u, more):
                            if more:
                                normed(b + 1, 1 - u)
                            act.wait_ge(turned, ready(b))
                            act.wait_ge(product, free(b))
                            nc.scalar.copy(hT[:, u, :, :], banks[:, u, 0:D].rearrange("p (f n) -> p f n", f=2)).then_inc(hT_ready, 1)
                            if act_mid:
                                act_mid(act, b, u, S)

                        normed(0, 0)
                        each_pair(act, NB, block)

                    @blk.tensor
                    def _(pe):
                        pe.sem_inc(turned, 2)
                        pe.sem_inc(product, 2)
                        if act_mid:
                            pe.sem_inc(mid_product, 2)
                        pe.wait_ge(w_in, 16)

                        def turn(b, u):
                            pe.wait_ge(h_ready, ready(b))
                            pe.wait_ge(hT_ready, free(b))
                            for f in range(2):
                                last = nc.tensor.transpose(banks[:, u, f * P:(f + 1) * P], h[:, u, f * P:(f + 1) * P], ident)
                            last.then_inc(turned, 1)

                        def block(b, u, more):
                            if more:
                                turn(b + 1, 1 - u)
                            pe.wait_ge(hT_ready, ready(b))
                            pe_mm(pe, b, u, S)

                        turn(0, 0)
                        each_pair(pe, NB, block)

                    @blk.vector
                    def _(dve):
                        dve.sem_inc(row_ready, 2)
                        norm_coefs(dve, tag, work, root_ready, steps)
                        for c, value in row_init:
                            nc.vector.memset(row[:, :, c:c + 1], value)
                        if load_extra:
                            dve.wait_ge(extra_in, 16)

                        def block(b, u, _):
                            dve.wait_ge(product, ready(b))
                            if not isinstance(b, int) or b > 1:
                                dve.wait_ge(row_free[u], (b - u) * 8)
                            dve_row(dve, b, u, S)

                        each_pair(dve, NB, block, 2)

        def qkv_mm(pe, b, u, S):
            pe.wait_ge(S["row_ready"], free(b))
            w, hT = S["w"], S["hT"]
            for bank, c0, c1 in ((2 + 2 * u, 0, 2 * D), (3 + 2 * u, 2 * D, 3 * D)):
                for k in range(2):
                    last = nc.tensor.matmul(banks[:, bank, 0:c1 - c0], hT[:, u, k, :], w[:, 3 * D * k + c0:3 * D * k + c1],
                                            start=(k == 0), stop=(k == 1))
            last.then_inc(S["product"], 1)

        def qkv_row(dve, b, u, S):
            bias, qk = S["extra"]
            row, chain = S["row"], S["chain"]
            v = nc.vector
            v.tensor_tensor(qk[:, u, :], banks[:, 2 + 2 * u, 0:2 * D], bias[:, 0:2 * D], ALU.add).then_inc(chain, 1)
            dve.wait_ge(S["row_taken"], free(b))
            v.tensor_tensor(row[:, u, 0:D], banks[:, 3 + 2 * u, 0:D], bias[:, 2 * D:3 * D], ALU.add)
            dve.wait_ge(chain, 2 * b + 1)
            v.scalar_tensor_tensor(qk[:, u, 0:D], qk[:, u, 0:D], float(HEAD_DIM) ** -0.5, qk[:, u, D:2 * D], ALU.mult, ALU.mult).then_inc(chain, 1)
            dve.wait_ge(chain, 2 * b + 2)
            v.tensor_reduce(row[:, u, D:ROW0], qk[:, u, 0:D].rearrange("p (h c) -> p h c", h=HEADS), AX_X, ALU.add).then_inc(S["row_ready"], 1)

        def keep_scores(pool, b, u, S):
            pool.wait_ge(S["row_ready"], ready(b))
            nc.gpsimd.tensor_copy(scores[:, bass.ds(b, 1), :].squeeze(1), S["row"][:, u, D:ROW0]).then_inc(S["row_taken"], 1)

        def qkv_alloc(st):
            return sb(st, "qkv_bias", [P, 3 * D]), sb(st, "qk", [P, 2, 2 * D])

        def qkv_load(sp, extra, done):
            sp.dma_start(extra[0][:, :], inp["bqkv"].partition_broadcast(P)).then_inc(done, 16)

        def filter_alloc(st):
            return sb(st, "mid", [P, 2, P])

        def filter_mm(pe, b, u, S):
            w, hT = S["w"], S["hT"]
            pe.wait_ge(S["mid_ready"], free(b))
            for k in range(2):
                last = nc.tensor.matmul(banks[:, 2 + u, 0:P], w[:, k * FILTERS:(k + 1) * FILTERS], hT[:, u, k, :], start=(k == 0), stop=(k == 1))
            last.then_inc(S["mid_product"], 1)
            pe.wait_ge(S["mid_ready"], ready(b))
            pe.wait_ge(S["row_ready"], free(b))
            nc.tensor.matmul(banks[:, 4 + u, 0:FILTERS], S["extra"][:, u, :], w[:, 2 * FILTERS:3 * FILTERS], start=True, stop=True).then_inc(S["product"], 1)

        def filter_mid(act, b, u, S):
            act.wait_ge(S["mid_product"], ready(b))
            act.wait_ge(S["product"], free(b))
            nc.scalar.activation(S["extra"][:, u, :], banks[:, 2 + u, 0:P], ACT.Identity, bias=col("b_n2m")).then_inc(S["mid_ready"], 1)

        def filter_row(dve, b, u, S):
            nc.vector.tensor_copy(S["row"][:, u, :], banks[:, 4 + u, 0:FILTERS]).then_inc(S["row_ready"], 1)

        def wn_alloc(st):
            return sb(st, "wn_rows", [P, 2 * D]), sb(st, "wn_junk", [P, 2, D])

        def wn_load(sp, extra, done):
            sp.dma_start(extra[0][:, :], inp["bn_attn"].partition_broadcast(P)).then_inc(done, 16)

        def wn_mm(pe, b, u, S):
            pe.wait_ge(S["row_ready"], free(b))
            for k in range(2):
                last = nc.tensor.matmul(banks[:, 2 + u, 0:D], S["hT"][:, u, k, :], S["w"][:, k * D:(k + 1) * D], start=(k == 0), stop=(k == 1))
            last.then_inc(S["product"], 1)

        def wn_row(dve, b, u, S):
            vectors, junk = S["extra"]
            row, chain = S["row"], S["chain"]
            nc.vector.tensor_tensor(row[:, u, 0:D], banks[:, 2 + u, 0:D], vectors[:, 0:D], ALU.add).then_inc(chain, 1)
            dve.wait_ge(chain, b + 1)
            nc.vector.scalar_tensor_tensor(junk[:, u, :], row[:, u, 0:D], 1.0, vectors[:, D:2 * D], ALU.mult, ALU.mult,
                                           accum_out=row[:, u, D + 1:D + 2]).then_inc(S["row_ready"], 1)

        gcn_mm = wn_mm

        def gcn_row(dve, b, u, S):
            dve.wait_ge(S["row_taken"], free(b))
            nc.vector.tensor_scalar(S["row"][:, u, :], banks[:, 2 + u, 0:D], dinv[:, bass.ds(b, 1)], None, ALU.mult).then_inc(S["row_ready"], 1)

        def keep_own(pool, b, u, S):
            pool.wait_ge(S["row_ready"], ready(b))
            nc.gpsimd.tensor_copy(acc[:, bass.ds(b, 1), 0:D].squeeze(1), S["row"][:, u, :]).then_inc(S["row_taken"], 1)

        def gather_batches(pool, table, width, rows, stage, staged, gathered, summed_tile, ahead):
            def gather(n, u):
                pool.wait_ge(summed_tile, summed(n - RING, G - 1))
                nc.gpsimd.tensor_copy(stage[:, u, :], src_idx[:, bass.ds(n * G, G)]).then_inc(staged, 1)
                pool.wait_ge(staged, n + 1)
                pool.sem_inc(carriers, 1)
                for q in range(G):
                    nc.gpsimd.indirect_dma_start(out=rows[:, u, q, 0:width], out_offset=None, in_=table,
                                                 in_offset=bass.IndirectOffsetOnAxis(ap=stage[:, u, q:q + 1], axis=0)).then_inc(gathered[u], 16)

            for n in range(ahead):
                gather(n, n)
            with pool.Fori(0, TURNS) as i:
                for r in range(RING):
                    gather(i * RING + r + ahead, (r + ahead) % RING)
            for u in range(RING):
                pool.wait_ge(gathered[u], 16 * G * (TURNS + (u < ahead)))

        def arrived(n, u):
            return (n - u) * (16 * G // RING) + 16 * G

        def load_blocks(engine, n):
            return nc.values_load_multi_w_load_instructions(
                step_block[0:1, bass.ds(n * G, G)], engines=[engine], min_val=0, max_val=NB - 1,
                skip_runtime_bounds_check_because="clamped when they were made")[1]

        def summed(j, q):
            return (j + RING) * G + q + 1

        def sum_tile(pe, j, q, onehot, rows, summed_tile, added, width):
            pe.wait_ge(added, j * G + q + 1)
            nc.tensor.matmul(banks[:, 2 + q % 4, 0:width], onehot, rows, start=True, stop=True).then_inc(summed_tile, 1)

        def add_tile(dve, j, q, block, summed_tile, added, width):
            dve.wait_ge(summed_tile, summed(j, q))
            dve.wait_ge(added, j * G + q + 4)
            at = acc[:, bass.ds(block, 1), 0:width].squeeze(1)
            nc.vector.tensor_tensor(at, at, banks[:, 2 + q % 4, 0:width], ALU.add).then_inc(added, 1)

        def softmax_edges(tag, table, row_w, sum_w, heads):
            many = heads > 1
            slope = ATT0_SLOPE if many else ATT2_SLOPE
            GH = G * heads
            ring_w = max(row_w, sum_w)
            st = ExitStack()
            with st:
                rows = sb(st, f"{tag}_rows", [P, RING, G, ring_w])
                stage = sb(st, f"{tag}_stage", [P, RING, G], I32)
                hot = sb(st, f"{tag}_hot", [P, RING, G, P])
                apart = sb(st, f"{tag}_apart", [P, G, P])
                restart = sb(st, f"{tag}_restart", [heads, 2, SLOTS + 1], BF16)
                maxes = sb(st, f"{tag}_maxes", [heads, SLOTS])
                val = sb(st, f"{tag}_val", [P, GH])
                sums = sb(st, f"{tag}_sums", [P, 3, GH])
                leaky = sb(st, f"{tag}_leaky", [P, RING, 3, GH])
                power = sb(st, f"{tag}_power", [P, 2, GH])
                scale_to = sb(st, f"{tag}_scale_to", [P, heads])
                ends = sb(st, f"{tag}_ends", [P, RING, 2, heads])
                if many:
                    hotT = sb(st, f"{tag}_hotT", [P, G, P])
                    at_dst = sb(st, f"{tag}_at_dst", [P, GH])
                else:
                    weight = sb(st, f"{tag}_weight", [P, RING, G])
                    weighted_hot = sb(st, f"{tag}_weighted_hot", [P, 2, G, P])
                gathered = [sem(f"{tag}_gathered{u}") for u in range(RING)]
                restart_in = [sem(f"{tag}_restart_in{u}") for u in range(2)]
                (staged, apart_ready, hot_ready, val_ready, val_turned, scan_fwd, scan_ready, max_turned, leaky_ready, power_ready, ends_ready, exp_ready,
                 weighted, delta_ready, scale_ready, scaled, summed_tile, added, logit_ready) = (sem(f"{tag}_{n}") for n in (
                     "staged", "apart_ready", "hot_ready", "val_ready", "val_turned", "scan_fwd", "scan_ready", "max_turned", "leaky_ready",
                     "power_ready", "ends_ready", "exp_ready", "weighted", "delta_ready", "scale_ready", "scaled", "summed_tile", "added", "logit_ready"))
                if many:
                    hotT_psum, hotT_ready, dst_scores, sums_ready = (sem(f"{tag}_{n}") for n in (
                        "hotT_psum", "hotT_ready", "dst_scores", "sums_ready"))
                scan_psum = banks[0:heads, 0:2, :].rearrange("h b e -> h (b e)")
                DST_AT, MAX_AT = 0, 128

                with nc.Block() as blk:
                    @blk.gpsimd
                    def _(pool):
                        gather_batches(pool, table, row_w, rows, stage, staged, gathered, summed_tile, 2)

                    @blk.sync
                    def _(sp):
                        def load(n, u):
                            sp.wait_ge(scan_ready, free(n))
                            sp.sem_inc(carriers, 1)
                            sp.dma_start(restart[:, u, :], restart_line[bass.ds(n * SLOTS, SLOTS + 1)].partition_broadcast(heads)).then_inc(restart_in[u], 16)

                        load(0, 0)
                        with sp.Fori(0, BATCHES // 2) as i:
                            load(2 * i + 1, 1)
                            load(2 * i + 2, 0)
                        sp.wait_ge(restart_in[0], 16 * (BATCHES // 2 + 1))
                        sp.wait_ge(restart_in[1], 16 * (BATCHES // 2))

                    @blk.scalar
                    def _(act):
                        def one_hot(n, u):
                            if not isinstance(n, int) or n > 0:
                                act.wait_ge(hot_ready, n)
                            for q in range(G):
                                last = nc.scalar.activation(apart[:, q, :], iota_n, ACT.Abs, bias=dst_loc[:, bass.ds(n * G + q, 1)], scale=-1.0)
                            last.then_inc(apart_ready, 1)
                            act.wait_ge(apart_ready, n + 1)
                            nc.scalar.activation(hot[:, u, :, :], apart[:, :, :], ACT.Relu, bias=ones[:, 0:1], scale=-1.0).then_inc(hot_ready, 1)

                        def keep_hotT(n):
                            for g in range(G // 4):
                                act.wait_ge(hotT_psum, n * (G // 4) + g + 1)
                                act.wait_ge(dst_scores, n)
                                nc.scalar.copy(hotT[:, 4 * g:4 * g + 4, :], banks[:, 6, :].rearrange("p (q e) -> p q e", q=4)).then_inc(hotT_ready, 1)

                        def exponent(n, u):
                            act.wait_ge(power_ready, n + 1)
                            if many:
                                to = rows[:, u, :, D:D + 2 * HEADS].rearrange("p t (c h) -> p c t h", c=2)
                                nc.scalar.activation(to, power[:, :, :].rearrange("p c (t h) -> p c t h", t=G), ACT.Exp).then_inc(exp_ready, 1)
                            else:
                                nc.scalar.activation(weight[:, u, :], power[:, 0, :], ACT.Exp).then_inc(exp_ready, 1)
                                act.wait_ge(hot_ready, n + 1)
                                act.wait_ge(exp_ready, n + 1)
                                act.wait_ge(summed_tile, summed(n - 2, G - 1))
                                for q in range(G):
                                    nc.scalar.activation(weighted_hot[:, u % 2, q, :], hot[:, u, q, :], ACT.Copy, scale=weight[:, u, q:q + 1]).then_inc(weighted, 1)
                            act.wait_ge(delta_ready, n + 1)
                            act.wait_ge(scaled, n)
                            nc.scalar.activation(scale_to[:, :], banks[:, 6, 0:heads], ACT.Exp).then_inc(scale_ready, 1)

                        for n in range(3):
                            one_hot(n, n)
                        act.wait_ge(hot_ready, 3)
                        if many:
                            keep_hotT(0)
                            keep_hotT(1)
                        exponent(0, 0)
                        if many:
                            keep_hotT(2)
                        with act.Fori(0, TURNS) as i:
                            for r in range(RING):
                                j = i * RING + r
                                one_hot(j + 3, (r + 3) % RING)
                                exponent(j + 1, (r + 1) % RING)
                                if many:
                                    keep_hotT(j + 3)

                    @blk.tensor
                    def _(pe):
                        pe.sem_inc(summed_tile, RING * G)

                        def turn_hot(n, u):
                            pe.wait_ge(hot_ready, n + 1)
                            if not isinstance(n, int) or n > 1:
                                pe.wait_ge(scale_ready, n - 1)
                            for g in range(G // 4):
                                pe.wait_ge(hotT_ready, n * (G // 4) + g)
                                for q in range(4 * g, 4 * g + 4):
                                    last = nc.tensor.transpose(banks[:, 6, (q % 4) * P:(q % 4 + 1) * P], hot[:, u, q, :], ident)
                                last.then_inc(hotT_psum, 1)

                        def dst_side(n):
                            blocks = load_blocks(PE_ENGINE, n)
                            pe.wait_ge(logit_ready, n)
                            for q in range(G):
                                if q % 4 == 0:
                                    pe.wait_ge(hotT_ready, n * (G // 4) + q // 4 + 1)
                                last = nc.tensor.matmul(banks[:, 7, DST_AT + q * heads:DST_AT + (q + 1) * heads], hotT[:, q, :],
                                                        scores[:, bass.ds(blocks[q], 1), :].squeeze(1), start=True, stop=True)
                            last.then_inc(dst_scores, 1)

                        def turn_val(n):
                            pe.wait_ge(val_ready, n + 1)
                            for q in range(G):
                                last = nc.tensor.transpose(banks[0:heads, q // 4, (q % 4) * P:(q % 4 + 1) * P], val[:, q * heads:(q + 1) * heads], ident)
                            last.then_inc(val_turned, 1)

                        def turn_max(n):
                            pe.wait_ge(scan_ready, ready(n))
                            pe.sem_inc(carriers, 1)
                            for q in range(G):
                                last = nc.tensor.transpose(banks[:, 7, MAX_AT + q * heads:MAX_AT + (q + 1) * heads],
                                                           maxes[:, q * P:(q + 1) * P], ident[0:heads, 0:heads])
                            last.then_inc(max_turned, 1)

                        def delta(n, u):
                            pe.wait_ge(hot_ready, n + 1)
                            pe.wait_ge(ends_ready, n + 1)
                            pe.wait_ge(scale_ready, n)
                            before, first = hot[:, (u - 1) % RING, G - 1, :], hot[:, u, 0, :]
                            nc.tensor.matmul(banks[:, 6, 0:heads], before, ends[:, u, 1, :], start=True, stop=False)
                            nc.tensor.matmul(banks[:, 6, 0:heads], first, ends[:, u, 0, :], start=False, stop=True).then_inc(delta_ready, 1)

                        def sums_of(j, u, q):
                            if many:
                                if q == 0:
                                    pe.wait_ge(weighted, j + 1)
                                by = hot[:, u, q, :]
                            else:
                                pe.wait_ge(weighted, j * G + q + 1)
                                by = weighted_hot[:, u % 2, q, :]
                            sum_tile(pe, j, q, by, rows[:, u, q, 0:sum_w], summed_tile, added, sum_w)

                        if many:
                            for n in range(2):
                                turn_hot(n, n)
                                dst_side(n)
                                if n == 0:
                                    turn_val(0)
                        else:
                            turn_val(0)
                        turn_max(0)
                        delta(0, 0)
                        turn_val(1)
                        if many:
                            turn_hot(2, 2)
                        with pe.Fori(0, TURNS) as i:
                            for r in range(RING):
                                j, u, un = i * RING + r, r, (r + 1) % RING
                                for q in range(4):
                                    sums_of(j, u, q)
                                if many:
                                    dst_side(j + 2)
                                turn_max(j + 1)
                                for q in range(4, G):
                                    sums_of(j, u, q)
                                delta(j + 1, un)
                                turn_val(j + 2)
                                if many:
                                    turn_hot(j + 3, (r + 3) % RING)

                    @blk.vector
                    def _(dve):
                        v = nc.vector
                        dve.sem_inc(scan_ready, 2)
                        dve.sem_inc(added, 4)
                        v.memset(maxes[:, :], 0.0).then_inc(scan_fwd, 1)
                        v.memset(leaky[:, :, :, :], 0.0)
                        v.memset(hot[:, RING - 1, :, :], 0.0)
                        if many:
                            v.memset(rows[:, :, :, ACC_W - 1:ACC_W], 1.0)
                        v.memset(ends[:, :, :, :], 0.0).then_inc(leaky_ready, 1)
                        dve.wait_ge(leaky_ready, 1)

                        def value(n, u):
                            dve.wait_ge(gathered[u], arrived(n, u))
                            if many:
                                dve.wait_ge(dst_scores, n + 1)
                                dst = banks[:, 7, DST_AT:DST_AT + GH]
                                v.tensor_tensor(val[:, :].rearrange("p (t h) -> p t h", t=G), rows[:, u, :, D:ROW0],
                                                dst.rearrange("p (t h) -> p t h", t=G), ALU.max).then_inc(val_ready, 1)
                                v.tensor_copy(at_dst[:, :], dst).then_inc(logit_ready, 1)
                            else:
                                v.tensor_tensor(sums[:, 0, :].unsqueeze(2), rows[:, u, :, D + 1:D + 2], edge_q[:, bass.ds(n * G, G)].unsqueeze(2), ALU.add).then_inc(logit_ready, 1)
                                dve.wait_ge(logit_ready, n + 1)
                                v.scalar_tensor_tensor(val[:, :], sums[:, 0, :], slope, sums[:, 0, :], ALU.mult, ALU.max).then_inc(val_ready, 1)

                        def scan_on(n, w):
                            dve.wait_ge(val_turned, n + 1)
                            dve.wait_ge(restart_in[w], (n - w) * 8 + 16)
                            dve.wait_ge(max_turned, n)
                            dve.wait_ge(scan_ready, n + 2)
                            v.tensor_tensor_scan(maxes[:, :], restart[:, w, 0:SLOTS], scan_psum, maxes[:, SLOTS - 1:SLOTS],
                                                 ALU.add, ALU.max).then_inc(scan_fwd, 1)

                        def scan_back(n, w):
                            dve.wait_ge(scan_fwd, n + 2)
                            back = maxes[:, :][:, ::-1]
                            v.tensor_tensor_scan(back, restart[:, w, 1:SLOTS + 1][:, ::-1], back, -BIG, ALU.add, ALU.max).then_inc(scan_ready, 1)

                        top_of = banks[:, 7, MAX_AT:MAX_AT + GH]

                        def take_max(n, u):
                            dve.wait_ge(max_turned, n + 1)
                            if many:
                                dve.wait_ge(logit_ready, n + 1)
                                v.tensor_tensor(sums[:, 0, :].rearrange("p (t h) -> p t h", t=G), rows[:, u, :, D:ROW0],
                                                at_dst[:, :].rearrange("p (t h) -> p t h", t=G), ALU.add)
                                v.tensor_tensor(sums[:, 1, :], at_dst[:, :], at_dst[:, :], ALU.add)
                                v.tensor_tensor(sums[:, 2, :], top_of, at_dst[:, :], ALU.add).then_inc(sums_ready, 1)
                            else:
                                dve.wait_ge(exp_ready, n)
                                v.tensor_tensor(power[:, 0, :], val[:, :], top_of, ALU.subtract).then_inc(power_ready, 1)
                                v.tensor_copy(leaky[:, u, 2, :], top_of).then_inc(leaky_ready, 1)

                        def leak(n, u):
                            dve.wait_ge(sums_ready, n + 1)
                            v.scalar_tensor_tensor(leaky[:, u, :, :], sums[:, :, :], slope, sums[:, :, :], ALU.mult, ALU.max).then_inc(leaky_ready, 1)

                        def powers(n, u):
                            dve.wait_ge(leaky_ready, n + 2)
                            highest = leaky[:, u, 2, :]
                            if many:
                                v.tensor_tensor(power[:, :, :], leaky[:, u, 0:2, :], highest.unsqueeze(1).broadcast_to([P, 2, GH]), ALU.subtract).then_inc(power_ready, 1)
                            v.tensor_scalar(ends[:, u, 0, :], highest[:, 0:heads], same_first[:, bass.ds(n, 1)], -1.0, ALU.mult, ALU.mult)
                            v.tensor_scalar(ends[:, u, 1, :], leaky[:, (u - 1) % RING, 2, GH - heads:GH], same_last[:, bass.ds(n, 1)], None, ALU.mult).then_inc(ends_ready, 1)

                        def weigh(n, u):
                            dve.wait_ge(exp_ready, n + 1)
                            to = rows[:, u, :, 0:D].rearrange("p t (h c) -> p t h c", h=HEADS)
                            e = rows[:, u, :, D:ROW0].unsqueeze(3).broadcast_to([P, G, HEADS, HEAD_DIM])
                            v.tensor_tensor(to, to, e, ALU.mult).then_inc(weighted, 1)

                        def rescale(j, block):
                            dve.wait_ge(scale_ready, j + 1)
                            dve.wait_ge(added, j * G + 4)
                            if many:
                                num = acc[:, bass.ds(block, 1), 0:D].squeeze(1).rearrange("p (h c) -> p h c", h=HEADS)
                                den = acc[:, bass.ds(block, 1), D:D + 2 * HEADS].squeeze(1).rearrange("p (c h) -> p c h", c=2)
                                v.tensor_tensor(num, num, scale_to[:, :].unsqueeze(2).broadcast_to([P, HEADS, HEAD_DIM]), ALU.mult)
                                v.tensor_tensor(den, den, scale_to[:, :].unsqueeze(1).broadcast_to([P, 2, HEADS]), ALU.mult).then_inc(scaled, 1)
                            else:
                                at = acc[:, bass.ds(block, 1), 0:sum_w].squeeze(1)
                                v.tensor_scalar(at, at, scale_to[:, 0:1], None, ALU.mult).then_inc(scaled, 1)
                            dve.wait_ge(scaled, j + 1)

                        value(0, 0)
                        dve.wait_ge(scan_fwd, 1)
                        scan_on(0, 0)
                        scan_back(0, 0)
                        take_max(0, 0)
                        if many:
                            leak(0, 0)
                        powers(0, 0)
                        value(1, 1)
                        if many:
                            weigh(0, 0)
                        with dve.Fori(0, TURNS) as i:
                            for r in range(RING):
                                j, u, un, w = i * RING + r, r, (r + 1) % RING, (r + 1) % 2
                                blocks = load_blocks(DVE_ENGINE, j)

                                def add(q):
                                    add_tile(dve, j, q, blocks[q], summed_tile, added, sum_w)

                                rescale(j, blocks[0])
                                scan_on(j + 1, w)
                                add(0)
                                scan_back(j + 1, w)
                                add(1)
                                add(2)
                                take_max(j + 1, un)
                                add(3)
                                if many:
                                    leak(j + 1, un)
                                add(4)
                                powers(j + 1, un)
                                add(5)
                                add(6)
                                value(j + 2, (r + 2) % RING)
                                add(7)
                                if many:
                                    weigh(j + 1, un)

        def plain_edges(tag, table, width, filtered):
            st = ExitStack()
            with st:
                rows = sb(st, f"{tag}_rows", [P, RING, G, width])
                stage = sb(st, f"{tag}_stage", [P, RING, G], I32)
                hot = sb(st, f"{tag}_hot", [P, RING, G, P])
                if filtered:
                    loc = sb(st, f"{tag}_loc", [P, RING, 2, G])
                    radial = sb(st, f"{tag}_radial", [P, RING, G, RADIAL])
                    edge_in = sb(st, f"{tag}_edge_in", [P, RING, G, EDGE_DIM])
                    radialT = sb(st, f"{tag}_radialT", [P, 2, P])
                    wr = sb(st, f"{tag}_wr", [P, 4 * FILTERS])
                    br = sb(st, f"{tag}_br", [1, 4 * FILTERS])
                    we = sb(st, f"{tag}_we", [P, 2 * EDGE_DIM])
                    attn = sb(st, f"{tag}_attn", [P, 2, P])
                    we_attn = sb(st, f"{tag}_we_attn", [P, EDGE_DIM])
                    be_attn = sb(st, f"{tag}_be_attn", [P, 1])
                    logit_part = sb(st, f"{tag}_logit_part", [P, G, EDGE_DIM])
                gathered = [sem(f"{tag}_gathered{u}") for u in range(RING)]
                staged, hot_ready, summed_tile, added = (sem(f"{tag}_{n}") for n in ("staged", "hot_ready", "summed_tile", "added"))
                if filtered:
                    radial_ready = [sem(f"{tag}_radial_in{u}") for u in range(RING)]
                    edge_ready = [sem(f"{tag}_edge_in{u}") for u in range(RING)]
                    (loc_ready, radial_psum, radialT_ready, filters, filtered_rows, logits, products, w_in, attn_ready,
                     we_attn_psum, we_attn_ready) = (sem(f"{tag}_{n}") for n in (
                         "loc_ready", "radial_psum", "radialT_ready", "filters", "filtered_rows", "logits", "products", "w_in",
                         "attn_ready", "we_attn_psum", "we_attn_ready"))

                with nc.Block() as blk:
                    @blk.gpsimd
                    def _(pool):
                        gather_batches(pool, table, width, rows, stage, staged, gathered, summed_tile, 1)

                    if filtered:
                        @blk.sync
                        def _(sp):
                            for to, name in ((wr, "w_r2m"), (br, "b_r2m"), (we, "we")):
                                sp.dma_start(to[:, :], inp[name]).then_inc(w_in, 16)

                            def load(n, u):
                                tiles = nc.values_load_multi_w_load_instructions(
                                    step_tile[0:1, bass.ds(n * G, G)], engines=[SP_ENGINE], min_val=0, max_val=TILES - 1,
                                    skip_runtime_bounds_check_because="clamped when they were made")[1]
                                sp.wait_ge(radial_psum, 2 * n + 2)
                                sp.sem_inc(carriers, 1)
                                sp.wait_ge(logits, n + 1)
                                sp.sem_inc(carriers, 1)
                                for q in range(G):
                                    sp.dma_start(radial[:, u, q, :], inp["edge_attr_32"][bass.ds(tiles[q] * P, P), :]).then_inc(radial_ready[u], 16)
                                    sp.dma_start(edge_in[:, u, q, :], inp["edge_attr_128"][bass.ds(tiles[q] * P, P), :]).then_inc(edge_ready[u], 16)

                            load(0, 0)
                            with sp.Fori(0, TURNS) as i:
                                for r in range(RING):
                                    load(i * RING + r + 1, (r + 1) % RING)
                            for u in range(RING):
                                sp.wait_ge(radial_ready[u], 16 * G * (TURNS + (u == 0)))
                                sp.wait_ge(edge_ready[u], 16 * G * (TURNS + (u == 0)))

                        @blk.scalar
                        def _(act):
                            def keep_radialT(n):
                                for g in range(2):
                                    act.wait_ge(radial_psum, 2 * RING + 2 * n + g + 1)
                                    act.wait_ge(filters, 2 * n + g)
                                    nc.scalar.copy(radialT[:, g, :], banks[:, 6 + g, 0:P]).then_inc(radialT_ready, 1)

                            keep_radialT(0)
                            with act.Fori(0, TURNS) as i:
                                for r in range(RING):
                                    keep_radialT(i * RING + r + 1)

                    @blk.tensor
                    def _(pe):
                        pe.sem_inc(summed_tile, RING * G)
                        if filtered:
                            pe.sem_inc(radial_psum, 2 * RING)
                            pe.wait_ge(w_in, 48)
                            pe.wait_ge(attn_ready, 1)
                            for c0, c1, rhs in ((0, EDGE_DIM, lambda k: we[:, k * EDGE_DIM:(k + 1) * EDGE_DIM]), (EDGE_DIM, EDGE_DIM + 1, lambda k: col("be", k))):
                                for k in range(2):
                                    last = nc.tensor.matmul(banks[:, 2, c0:c1], attn[:, k, :], rhs(k), start=(k == 0), stop=(k == 1))
                            last.then_inc(we_attn_psum, 1)
                            pe.wait_ge(we_attn_ready, 1)

                        def turn_radial(n, u):
                            pe.wait_ge(radial_ready[u], arrived(n, u))
                            for g in range(2):
                                pe.wait_ge(radialT_ready, 2 * n + g)
                                nc.tensor.transpose(banks[:, 6 + g, 0:P], radial[:, u, 4 * g:4 * g + 4, :].rearrange("p q c -> p (q c)"), ident).then_inc(radial_psum, 1)

                        def make_filters(n):
                            for g in range(2):
                                pe.wait_ge(filtered_rows, 2 * n + g)
                                pe.wait_ge(radialT_ready, 2 * n + g + 1)
                                nc.tensor.matmul(banks[:, g, :], ones[0:1, :], br[:, :], start=True, stop=False)
                                nc.tensor.matmul(banks[:, g, :], radialT[:, g, :], wr[:, :], start=False, stop=True).then_inc(filters, 1)

                        def sums_of(j, u, q):
                            if q == 0:
                                if filtered:
                                    pe.wait_ge(filtered_rows, 2 * j + 2)
                                else:
                                    pe.wait_ge(gathered[u], arrived(j, u))
                                pe.wait_ge(hot_ready, j + 1)
                            sum_tile(pe, j, q, hot[:, u, q, :], rows[:, u, q, :], summed_tile, added, width)

                        if filtered:
                            turn_radial(0, 0)
                            make_filters(0)
                        with pe.Fori(0, TURNS) as i:
                            for r in range(RING):
                                j, u, un = i * RING + r, r, (r + 1) % RING
                                for q in range(G // 2):
                                    sums_of(j, u, q)
                                if filtered:
                                    turn_radial(j + 1, un)
                                    make_filters(j + 1)
                                for q in range(G // 2, G):
                                    sums_of(j, u, q)

                    @blk.vector
                    def _(dve):
                        v = nc.vector
                        dve.sem_inc(added, 4)
                        if filtered:
                            dve.sem_inc(logits, RING)
                            v.memset(edge_q[:, (BATCHES + 1) * G:], 0.0)
                            for k in range(2):
                                last = v.tensor_scalar(attn[:, k, :], ones[:, :], col("attn", k), None, ALU.mult)
                            last.then_inc(attn_ready, 1)
                            dve.wait_ge(we_attn_psum, 1)
                            v.tensor_copy(we_attn[:, :], banks[:, 2, 0:EDGE_DIM])
                            v.tensor_copy(be_attn[:, :], banks[:, 2, EDGE_DIM:EDGE_DIM + 1]).then_inc(we_attn_ready, 1)
                            dve.wait_ge(we_attn_ready, 1)

                        def one_hot(n, u):
                            where = dst_loc[:, bass.ds(n * G, G)]
                            if not filtered:
                                v.tensor_tensor(hot[:, u, :, :], iota_n.unsqueeze(1).broadcast_to([P, G, P]),
                                                where.unsqueeze(2).broadcast_to([P, G, P]), ALU.is_equal).then_inc(hot_ready, 1)
                                return
                            v.tensor_copy(loc[:, u, 0, :], where)
                            v.tensor_copy(loc[:, u, 1, :], cutoff[:, bass.ds(n * G, G)]).then_inc(loc_ready, 1)
                            dve.wait_ge(loc_ready, n + 1)
                            for q in range(G):
                                last = v.tensor_scalar(hot[:, u, q, :], iota_n, loc[:, u, 0, q:q + 1], loc[:, u, 1, q:q + 1], ALU.is_equal, ALU.mult)
                            last.then_inc(hot_ready, 1)

                        def filter_batch(n, u):
                            dve.wait_ge(gathered[u], arrived(n, u))
                            for g in range(2):
                                dve.wait_ge(filters, 2 * n + g + 1)
                                to = rows[:, u, 4 * g:4 * g + 4, :]
                                v.tensor_tensor(to, to, banks[:, g, :].rearrange("p (q f) -> p q f", q=4), ALU.mult).then_inc(filtered_rows, 1)

                        def edge_logits(n, u):
                            dve.wait_ge(edge_ready[u], arrived(n, u))
                            v.tensor_tensor(logit_part[:, :, :], edge_in[:, u, :, :], we_attn[:, :].unsqueeze(1).broadcast_to([P, G, EDGE_DIM]), ALU.mult).then_inc(products, 1)
                            dve.wait_ge(products, n + 1)
                            v.tensor_reduce(edge_q[:, bass.ds(n * G, G)], logit_part[:, :, :], AX_X, ALU.add).then_inc(logits, 1)

                        one_hot(0, 0)
                        if filtered:
                            filter_batch(0, 0)
                            edge_logits(0, 0)
                        with dve.Fori(0, TURNS) as i:
                            for r in range(RING):
                                j, u, un = i * RING + r, r, (r + 1) % RING
                                blocks = load_blocks(DVE_ENGINE, j)
                                one_hot(j + 1, un)
                                for q in range(G // 2):
                                    add_tile(dve, j, q, blocks[q], summed_tile, added, width)
                                if filtered:
                                    filter_batch(j + 1, un)
                                    edge_logits(j + 1, un)
                                for q in range(G // 2, G):
                                    add_tile(dve, j, q, blocks[q], summed_tile, added, width)
                        if filtered:
                            dve.wait_ge(logits, BATCHES + 1 + RING)
                            v.tensor_scalar(edge_q[:, 0:(BATCHES + 1) * G], edge_q[:, 0:(BATCHES + 1) * G], be_attn[:, 0:1], None, ALU.add)

        def column_norm(dve, RT, part, whole, scaling, gamma, beta, steps, root_ready):
            v = nc.vector
            for f in range(2):
                with dve.Fori(0, BN_CHUNKS) as i:
                    v.bn_stats(part[:, f, bass.ds(i, 1), :].squeeze(1), RT[:, f, bass.ds(i * BN_CHUNK, BN_CHUNK)])
            n = 0

            def link(ins):
                nonlocal n
                n += 1
                ins.then_inc(steps, 1)
                dve.wait_ge(steps, n)

            link(v.memset(scaling[:, :, :], 0.0))
            for f in range(2):
                last = v.bn_aggr(whole[:, f, :], part[:, f, :, :].rearrange("p i s -> p (i s)"))
            link(last)
            dve.wait_ge(root_ready, 1)
            link(v.reciprocal(whole[:, :, 1], scaling[:, 0, :]))
            link(v.tensor_tensor(scaling[:, 0, :], whole[:, :, 1], cols[:, COLS[gamma][0]:COLS[gamma][1]], ALU.mult))
            link(v.tensor_tensor(whole[:, :, 0], whole[:, :, 0], scaling[:, 0, :], ALU.mult))
            link(v.tensor_tensor(scaling[:, 1, :], cols[:, COLS[beta][0]:COLS[beta][1]], whole[:, :, 0], ALU.subtract))

        BN_VAR_STEP, BN_STEP = 2, 6

        def column_root(act, whole, scaling, steps, root_ready):
            act.wait_ge(steps, BN_VAR_STEP)
            nc.scalar.activation(scaling[:, 0, :], whole[:, :, 1], ACT.Sqrt, bias=eps[:, 0:1]).then_inc(root_ready, 1)

        def layer0_tail():
            st = ExitStack()
            with st:
                RT = sb(st, "RT", [P, 2, N_PAD])
                part = sb(st, "bn_part", [P, 2, BN_CHUNKS, 6])
                whole = sb(st, "bn_whole", [P, 2, 2])
                scaling = [sb(st, f"bn_scaling{i}", [P, 2, 2]) for i in range(2)]
                attention_out(RT, part, whole, scaling[0])
                feed_forward(RT, part, whole, scaling)
                add_layer0(RT, scaling[1])

        def attention_out(RT, part, whole, scaling):
            st = ExitStack()
            with st:
                wo = sb(st, "wo", [P, 2 * D])
                values = sb(st, "values", [P, 2, D])
                own = sb(st, "own", [P, NB, HEADS])
                share = sb(st, "share", [P, NB, HEADS])
                per_node = sb(st, "per_node", [P, 3, NB])
                att = sb(st, "att", [P, 2, D])
                att_sum = sb(st, "att_sum", [P, 2, D])
                h = sb(st, "ao_h", [P, 2, D])
                attT = sb(st, "attT", [P, 2, 2, P])
                w_in, steps, root = sem("ao_w_in"), sem("ao_steps"), sem("ao_root")
                values_in = [sem(f"ao_values_in{u}") for u in range(2)]
                own_part, with_sum, att_ready, turned, attT_ready, h_ready, product, kept = (sem(f"ao_{n}") for n in (
                    "own_part", "with_sum", "att_ready", "turned", "attT_ready", "h_ready", "product", "kept"))
                bn_steps, bn_root = sem("ao_bn_steps"), sem("ao_bn_root")
                DEG_STEP, LAST_STEP = 2, 6

                with nc.Block() as blk:
                    @blk.sync
                    def _(sp):
                        sp.dma_start(wo[:, :], inp["wo"]).then_inc(w_in, 16)

                        def load(b, u, _):
                            sp.wait_ge(own_part, free(b))
                            sp.sem_inc(carriers, 1)
                            sp.dma_start(values[:, u, :], node_rows(table0, b)[:, 0:D]).then_inc(values_in[u], 16)

                        each_pair(sp, NB, load)

                    @blk.scalar
                    def _(act):
                        act.sem_inc(attT_ready, 2)
                        act.sem_inc(h_ready, 2)
                        act.sem_inc(kept, 2)
                        act.wait_ge(steps, DEG_STEP)
                        nc.scalar.activation(per_node[:, 2, :], degree[:, :], ACT.Sqrt, bias=ones[:, 0:1]).then_inc(root, 1)

                        def normed(b, u):
                            act.wait_ge(product, free(b))
                            nc.scalar.activation(h[:, u, :], X[:, bass.ds(b, 1), :].squeeze(1), ACT.Relu,
                                                 bias=nbias[:, bass.ds(b, 1)], scale=rstd[:, bass.ds(b, 1)]).then_inc(h_ready, 1)

                        def block(b, u, _):
                            normed(b, u)
                            act.wait_ge(turned, ready(b))
                            nc.scalar.copy(attT[:, u, :, :], banks[:, u, 0:D].rearrange("p (f n) -> p f n", f=2)).then_inc(attT_ready, 1)
                            act.wait_ge(product, ready(b))
                            for f in range(2):
                                last = nc.scalar.activation(RT[:, f, bass.ds(b * P, P)], banks[:, 2 + u, f * P:(f + 1) * P], ACT.Identity, bias=col("bo", f))
                            last.then_inc(kept, 1)

                        each_pair(act, NB, block)
                        column_root(act, whole, scaling, bn_steps, bn_root)

                    @blk.tensor
                    def _(pe):
                        pe.sem_inc(turned, 2)
                        pe.sem_inc(product, 2)
                        pe.wait_ge(w_in, 16)

                        def turn(b, u):
                            pe.wait_ge(att_ready, ready(b))
                            pe.wait_ge(attT_ready, free(b))
                            for f in range(2):
                                last = nc.tensor.transpose(banks[:, u, f * P:(f + 1) * P], att[:, u, f * P:(f + 1) * P], ident)
                            last.then_inc(turned, 1)

                        def block(b, u, more):
                            if more:
                                turn(b + 1, 1 - u)
                            pe.wait_ge(attT_ready, ready(b))
                            pe.wait_ge(h_ready, ready(b))
                            pe.wait_ge(kept, free(b))
                            for f in range(2):
                                to = banks[:, 2 + u, f * P:(f + 1) * P]
                                for k in range(2):
                                    nc.tensor.matmul(to, wo[:, k * D + f * P:k * D + (f + 1) * P], attT[:, u, k, :], start=(k == 0), stop=False)
                                last = nc.tensor.matmul(to, h[:, u, f * P:(f + 1) * P], ident, start=False, stop=True)
                            last.then_inc(product, 1)

                        turn(0, 0)
                        each_pair(pe, NB, block)

                    @blk.vector
                    def _(dve):
                        v = nc.vector
                        dve.sem_inc(own_part, 2)
                        dve.sem_inc(att_ready, 2)
                        n = 0

                        def link(ins):
                            nonlocal n
                            n += 1
                            ins.then_inc(steps, 1)
                            dve.wait_ge(steps, n)

                        v.tensor_copy(degree[:, :], acc[:, :, ACC_W - 1])
                        link(v.tensor_scalar(per_node[:, 0, :], acc[:, :, ACC_W - 1], 1.0, None, ALU.max))
                        v.tensor_scalar(per_node[:, 1, :], degree[:, :], 0.0, None, ALU.is_equal)
                        link(v.reciprocal(per_node[:, 0, :], per_node[:, 0, :]))
                        link(v.tensor_tensor(own[:, :, :], acc[:, :, D + HEADS:D + 2 * HEADS], per_node[:, 0, :].unsqueeze(2).broadcast_to([P, NB, HEADS]), ALU.mult))
                        link(v.tensor_tensor(own[:, :, :], own[:, :, :], per_node[:, 1, :].unsqueeze(2).broadcast_to([P, NB, HEADS]), ALU.add))
                        link(v.tensor_tensor(share[:, :, :], acc[:, :, D:ROW0], own[:, :, :], ALU.add))
                        dve.wait_ge(root, 1)
                        v.reciprocal(dinv[:, :], per_node[:, 2, :])
                        link(v.reciprocal(share[:, :, :], share[:, :, :]))

                        def by_head(ap, b):
                            return ap[:, bass.ds(b, 1), :].squeeze(1).unsqueeze(2).broadcast_to([P, HEADS, HEAD_DIM])

                        def split(ap):
                            return ap.rearrange("p (h c) -> p h c", h=HEADS)

                        def block(b, u, _):
                            dve.wait_ge(values_in[u], (b - u) * 8 + 16)
                            v.tensor_tensor(split(att_sum[:, u, :]), split(values[:, u, :]), by_head(own, b), ALU.mult).then_inc(own_part, 1)
                            dve.wait_ge(own_part, ready(b))
                            v.tensor_tensor(att_sum[:, u, :], att_sum[:, u, :], acc[:, bass.ds(b, 1), 0:D].squeeze(1), ALU.add).then_inc(with_sum, 1)
                            dve.wait_ge(with_sum, b + 1)
                            dve.wait_ge(turned, free(b))
                            v.tensor_tensor(split(att[:, u, :]), split(att_sum[:, u, :]), by_head(share, b), ALU.mult).then_inc(att_ready, 1)

                        each_pair(dve, NB, block)
                        dve.wait_ge(kept, ready(NB - 1))
                        column_norm(dve, RT, part, whole, scaling, "bn1_g", "bn1_b", bn_steps, bn_root)

        def feed_forward(RT, part, whole, scaling):
            st = ExitStack()
            with st:
                w1 = sb(st, "w1", [P, 2 * FF])
                w2 = sb(st, "w2", [P, 4 * D])
                hidden = sb(st, "hidden", [P, 2, 4, CHUNK])
                w_in = sem("ff_w_in")
                normed, up, hidden_ready, down, merged = (sem(f"ff_{n}") for n in ("normed", "up", "hidden_ready", "down", "merged"))
                bn_steps, bn_root = sem("ff_bn_steps"), sem("ff_bn_root")
                M = FF // P

                with nc.Block() as blk:
                    @blk.sync
                    def _(sp):
                        sp.dma_start(w1[:, :], inp["w1"]).then_inc(w_in, 16)
                        sp.dma_start(w2[:, :], inp["w2"]).then_inc(w_in, 16)

                    @blk.scalar
                    def _(act):
                        act.sem_inc(hidden_ready, M)

                        def norm(c):
                            for f in range(2):
                                at = RT[:, f, bass.ds(c * CHUNK, CHUNK)]
                                last = nc.scalar.activation(at, at, ACT.Identity, bias=scaling[0][:, 1, f:f + 1], scale=scaling[0][:, 0, f:f + 1])
                            last.then_inc(normed, 1)

                        def chunk(c, u, more):
                            if more:
                                norm(c + 1)
                            for m in range(M):
                                act.wait_ge(up, c * M + m + 1)
                                act.wait_ge(down, free(c))
                                nc.scalar.activation(hidden[:, u, m, :], banks[:, m, 0:CHUNK], ACT.Relu, bias=col("b1", m)).then_inc(hidden_ready, 1)

                        norm(0)
                        each_pair(act, CHUNKS, chunk)
                        column_root(act, whole, scaling[1], bn_steps, bn_root)

                    @blk.tensor
                    def _(pe):
                        pe.sem_inc(down, 2)
                        pe.wait_ge(w_in, 32)

                        def go_up(c):
                            pe.wait_ge(normed, c + 1)
                            for m in range(M):
                                pe.wait_ge(hidden_ready, c * M + m + 1)
                                for k in range(2):
                                    last = nc.tensor.matmul(banks[:, m, 0:CHUNK], w1[:, k * FF + m * P:k * FF + (m + 1) * P],
                                                            RT[:, k, bass.ds(c * CHUNK, CHUNK)], start=(k == 0), stop=(k == 1))
                                last.then_inc(up, 1)

                        def chunk(c, u, more):
                            if more:
                                go_up(c + 1)
                            pe.wait_ge(hidden_ready, (c + 1) * M + M)
                            pe.wait_ge(merged, free(c))
                            for f in range(2):
                                for m in range(M):
                                    last = nc.tensor.matmul(banks[:, 4 + 2 * u + f, 0:CHUNK], w2[:, m * D + f * P:m * D + (f + 1) * P],
                                                            hidden[:, u, m, :], start=(m == 0), stop=(m == M - 1))
                            last.then_inc(down, 1)

                        go_up(0)
                        each_pair(pe, CHUNKS, chunk)

                    @blk.vector
                    def _(dve):
                        v = nc.vector
                        dve.sem_inc(merged, 2)

                        def chunk(c, u, _):
                            dve.wait_ge(down, ready(c))
                            for f in range(2):
                                at = RT[:, f, bass.ds(c * CHUNK, CHUNK)]
                                last = v.scalar_tensor_tensor(at, banks[:, 4 + 2 * u + f, 0:CHUNK], col("b2", f), at, ALU.add, ALU.add)
                            last.then_inc(merged, 1)

                        each_pair(dve, CHUNKS, chunk)
                        dve.wait_ge(merged, ready(CHUNKS - 1))
                        column_norm(dve, RT, part, whole, scaling[1], "bn2_g", "bn2_b", bn_steps, bn_root)

        def add_layer0(RT, scaling):
            st = ExitStack()
            with st:
                normed = sb(st, "al_normed", [P, 2, 2, P])
                normed_ready, turned, updated = sem("al_normed_ready"), sem("al_turned"), sem("al_updated")
                with nc.Block() as blk:
                    @blk.scalar
                    def _(act):
                        act.sem_inc(normed_ready, 2)

                        def block(b, u, _):
                            act.wait_ge(turned, free(b))
                            for f in range(2):
                                last = nc.scalar.activation(normed[:, u, f, :], RT[:, f, bass.ds(b * P, P)], ACT.Identity,
                                                            bias=scaling[:, 1, f:f + 1], scale=scaling[:, 0, f:f + 1])
                            last.then_inc(normed_ready, 1)

                        each_pair(act, NB, block)

                    @blk.tensor
                    def _(pe):
                        pe.sem_inc(turned, 2)

                        def block(b, u, _):
                            pe.wait_ge(normed_ready, ready(b))
                            pe.wait_ge(updated, free(b))
                            for f in range(2):
                                last = nc.tensor.transpose(banks[:, u, f * P:(f + 1) * P], normed[:, u, f, :], ident)
                            last.then_inc(turned, 1)

                        each_pair(pe, NB, block)

                    @blk.vector
                    def _(dve):
                        dve.sem_inc(updated, 2)

                        def block(b, u, _):
                            dve.wait_ge(turned, ready(b))
                            add_to_x(dve, b, banks[:, u, 0:D], updated)

                        each_pair(dve, NB, block)

        def add_to_x(dve, b, what, updated):
            at = X[:, bass.ds(b, 1), :].squeeze(1)
            nc.vector.tensor_tensor(at, at, what, ALU.add).then_inc(updated, 1)
            dve.wait_ge(updated, ready(b))
            nc.vector.bn_stats(stats[:, bass.ds(b, 1), :].squeeze(1), at)

        def filter_out():
            st = ExitStack()
            with st:
                w = sb(st, "fo_w", [P, FILTERS + D])
                agg = sb(st, "fo_agg", [P, 2, FILTERS])
                aggT = sb(st, "fo_aggT", [P, 2, P])
                lin = sb(st, "fo_lin", [P, 2, P])
                w_in = sem("fo_w_in")
                agg_ready, turned, aggT_ready, lin_psum, lin_ready, product, updated = (sem(f"fo_{n}") for n in (
                    "agg_ready", "turned", "aggT_ready", "lin_psum", "lin_ready", "product", "updated"))
                with nc.Block() as blk:
                    @blk.sync
                    def _(sp):
                        sp.dma_start(w[:, :], inp["w_out1"]).then_inc(w_in, 16)

                    @blk.scalar
                    def _(act):
                        for s_ in (agg_ready, aggT_ready, lin_ready):
                            act.sem_inc(s_, 2)

                        def take(b, u):
                            act.wait_ge(turned, free(b))
                            nc.scalar.copy(agg[:, u, :], acc[:, bass.ds(b, 1), 0:FILTERS].squeeze(1)).then_inc(agg_ready, 1)

                        def block(b, u, more):
                            if more:
                                take(b + 1, 1 - u)
                            act.wait_ge(turned, ready(b))
                            act.wait_ge(lin_psum, free(b))
                            nc.scalar.copy(aggT[:, u, :], banks[:, u, 0:P]).then_inc(aggT_ready, 1)
                            act.wait_ge(lin_psum, ready(b))
                            act.wait_ge(product, free(b))
                            nc.scalar.activation(lin[:, u, :], banks[:, 2 + u, 0:P], ACT.Identity, bias=col("b_lin2")).then_inc(lin_ready, 1)

                        take(0, 0)
                        each_pair(act, NB, block)

                    @blk.tensor
                    def _(pe):
                        for s_ in (turned, lin_psum, product):
                            pe.sem_inc(s_, 2)
                        pe.wait_ge(w_in, 16)

                        def turn(b, u):
                            pe.wait_ge(agg_ready, ready(b))
                            pe.wait_ge(aggT_ready, free(b))
                            nc.tensor.transpose(banks[:, u, 0:P], agg[:, u, :], ident).then_inc(turned, 1)

                        def block(b, u, more):
                            if more:
                                turn(b + 1, 1 - u)
                            pe.wait_ge(aggT_ready, ready(b))
                            pe.wait_ge(lin_ready, free(b))
                            nc.tensor.matmul(banks[:, 2 + u, 0:P], w[:, 0:FILTERS], aggT[:, u, :], start=True, stop=True).then_inc(lin_psum, 1)
                            pe.wait_ge(lin_ready, ready(b))
                            pe.wait_ge(updated, free(b))
                            nc.tensor.matmul(banks[:, 4 + u, 0:D], lin[:, u, :], w[:, FILTERS:FILTERS + D], start=True, stop=True).then_inc(product, 1)

                        turn(0, 0)
                        each_pair(pe, NB, block)

                    @blk.vector
                    def _(dve):
                        dve.sem_inc(updated, 2)

                        def block(b, u, _):
                            dve.wait_ge(product, ready(b))
                            add_to_x(dve, b, banks[:, 4 + u, 0:D], updated)

                        each_pair(dve, NB, block)

        def gat_out():
            st = ExitStack()
            with st:
                share = sb(st, "go_share", [P, NB])
                part = sb(st, "go_part", [P, 2, D])
                steps, part_ready, updated = sem("go_steps"), sem("go_part_ready"), sem("go_updated")
                with nc.Block() as blk:
                    @blk.vector
                    def _(dve):
                        v = nc.vector
                        dve.sem_inc(updated, 2)
                        v.tensor_scalar(share[:, :], acc[:, :, D], 1e-16, None, ALU.add).then_inc(steps, 1)
                        dve.wait_ge(steps, 1)
                        v.reciprocal(share[:, :], share[:, :]).then_inc(steps, 1)
                        dve.wait_ge(steps, 2)

                        def block(b, u, _):
                            v.tensor_scalar(part[:, u, :], acc[:, bass.ds(b, 1), 0:D].squeeze(1), share[:, bass.ds(b, 1)], 0.0,
                                            ALU.mult, ALU.max).then_inc(part_ready, 1)
                            dve.wait_ge(part_ready, b + 1)
                            add_to_x(dve, b, part[:, u, :], updated)

                        each_pair(dve, NB, block)

        def gcn_out():
            st = ExitStack()
            with st:
                bias = sb(st, "gc_bias", [P, D])
                part = sb(st, "gc_part", [P, 2, D])
                bias_in, part_ready, updated, out_done = (sem(f"gc_{n}") for n in ("bias_in", "part_ready", "updated", "out_done"))
                with nc.Block() as blk:
                    @blk.sync
                    def _(sp):
                        sp.dma_start(bias[:, :], inp["b3"].partition_broadcast(P)).then_inc(bias_in, 16)
                        with sp.Fori(0, NB - 1) as b:
                            sp.wait_ge(updated, ready(b))
                            sp.sem_inc(carriers, 1)
                            sp.dma_start(node_rows(out, b), X[:, bass.ds(b, 1), :].squeeze(1)).then_inc(out_done, 16)
                        sp.wait_ge(updated, ready(NB - 1))
                        sp.dma_start(out[(NB - 1) * P:N_NODES, :], X[0:LAST, NB - 1, :]).then_inc(out_done, 16)
                        sp.wait_ge(out_done, 16 * NB)

                    @blk.vector
                    def _(dve):
                        v = nc.vector
                        dve.sem_inc(updated, 2)
                        dve.wait_ge(bias_in, 16)

                        def block(b, u, _):
                            v.scalar_tensor_tensor(part[:, u, :], acc[:, bass.ds(b, 1), 0:D].squeeze(1), dinv[:, bass.ds(b, 1)], bias[:, :],
                                                   ALU.mult, ALU.add).then_inc(part_ready, 1)
                            dve.wait_ge(part_ready, b + 1)
                            at = X[:, bass.ds(b, 1), :].squeeze(1)
                            v.scalar_tensor_tensor(at, part[:, u, :], 0.0, at, ALU.max, ALU.add).then_inc(updated, 1)

                        each_pair(dve, NB, block)

        node_stage("n0", inp["wqkv"], 6 * D, qkv_load, qkv_mm, qkv_row, None, keep_scores, table0, ROW0, (), qkv_alloc)
        softmax_edges("e0", table0, ROW0, ACC_W, HEADS)
        layer0_tail()
        layer_ends()

        node_stage("n1", inp["w_n2m"], 3 * FILTERS, None, filter_mm, filter_row, filter_mid, None, table1, FILTERS, (), filter_alloc)
        plain_edges("e1", table1, FILTERS, True)
        filter_out()
        layer_ends()

        node_stage("n2", inp["wn"], 2 * D, wn_load, wn_mm, wn_row, None, None, table2, ROW2, ((D, 1.0),), wn_alloc)
        softmax_edges("e2", table2, ROW2, D + 1, 1)
        gat_out()
        layer_ends()

        node_stage("n3", inp["w3"], 2 * D, None, gcn_mm, gcn_row, None, keep_own, table3, D, (), None)
        plain_edges("e3", table3, D, False)
        gcn_out()


def constants():
    c = np.zeros((P, CONST_W), np.float32)
    p = np.arange(P)

    def part(name):
        return c[:, CONST[name][0]:CONST[name][1]]

    part("iota_k")[:] = np.arange(STEPS)
    part("iota_n")[:] = p
    part("ident")[:] = np.eye(P)
    part("tile")[:] = np.arange(GROUPS) * P + p[:, None]
    part("p_first")[0] = 1
    part("p_last")[P - 1] = 1
    return c


def kernel(**inputs):
    import concourse.bacc as bacc
    from concourse.bass_utils import run_bass_kernel_spmd

    def a(name):
        return np.asarray(inputs[name])

    def padded(array, rows, value=0):
        fill = np.full((rows - array.shape[0],) + array.shape[1:], value, array.dtype)
        return np.ascontiguousarray(np.concatenate([array, fill]))

    def chunks(w):
        return np.ascontiguousarray(np.concatenate([w[k:k + P] for k in range(0, w.shape[0], P)], axis=1))

    def by_partition(name):
        return a(name).reshape(-1, P).T

    g, l1, l2 = "L0_gnn_", "L1_gnn_", "L2_gnn_"
    w_r2m = np.zeros((P, 4 * FILTERS), np.float32)
    for q in range(4):
        w_r2m[q * RADIAL:(q + 1) * RADIAL, q * FILTERS:(q + 1) * FILTERS] = a(l1 + "W_r2m").T
    arrays = {
        "const": constants(),
        "x": padded(a("x"), N_PAD),
        "src": padded(a("src"), E_PAD),
        "dst": padded(a("dst"), E_PAD + P, NO_NODE),
        "edge_weight": padded(a("edge_weight"), E_PAD),
        "edge_attr_32": padded(a("edge_attr_32"), TILES * P),
        "edge_attr_128": padded(a("edge_attr_128"), TILES * P),
        "cols": np.ascontiguousarray(np.concatenate([by_partition(n) for n in (
            g + "bo", g + "bn1_g", g + "bn1_b", g + "b1", g + "b2", g + "bn2_g", g + "bn2_b",
            l1 + "b_n2m", l1 + "b_lin2", l2 + "be", l2 + "attn")], axis=1)),
        "wqkv": chunks(np.concatenate([a(g + "Wq"), a(g + "Wk"), a(g + "Wv")], axis=1)),
        "bqkv": np.concatenate([a(g + "bq"), a(g + "bk"), a(g + "bv")]),
        "wo": chunks(a(g + "Wo")),
        "w1": chunks(a(g + "W1")),
        "w2": chunks(a(g + "W2")),
        "w_n2m": np.ascontiguousarray(np.concatenate([chunks(a(l1 + "W_n2m").T), a(l1 + "W_lin1").T], axis=1)),
        "w_r2m": w_r2m,
        "b_r2m": np.ascontiguousarray(np.concatenate([a(l1 + "b_r2m")] * 4)[None]),
        "w_out1": np.ascontiguousarray(np.concatenate([a(l1 + "W_lin2").T, a(l1 + "W_m2n").T], axis=1)),
        "wn": chunks(a(l2 + "Wn").T),
        "bn_attn": np.concatenate([a(l2 + "bn"), a(l2 + "attn").reshape(-1)]),
        "we": chunks(a(l2 + "We")),
        "w3": chunks(a("L3_gnn_W")),
        "b3": a("L3_gnn_b"),
    }
    nc = bacc.Bacc("TRN2", target_bir_lowering=False, num_devices=1)
    inp = {n: nc.dram_tensor(f"in_{n}", v.shape, mybir.dt.from_np(v.dtype), kind="ExternalInput").ap() for n, v in arrays.items()}
    out = nc.dram_tensor("out", (N_NODES, D), F32, kind="ExternalOutput").ap()
    build(nc, inp, out)
    r = run_bass_kernel_spmd(nc, [{f"in_{n}": v for n, v in arrays.items()}], core_ids=[0])
    return r.results[0]["out"]
```

```python
from contextlib import ExitStack

import numpy as np

import concourse.bass as bass
from concourse import mybir

F32 = mybir.dt.float32
BF16 = mybir.dt.bfloat16
I32 = mybir.dt.int32
ALU = mybir.AluOpType
ACT = mybir.ActivationFunctionType
AX_X = mybir.AxisListType.X
DVE_ENGINE = mybir.EngineType.DVE
PE_ENGINE = mybir.EngineType.PE
SP_ENGINE = mybir.EngineType.SP

P = 128
N_NODES, N_EDGES = 6250, 100000
D = 256
HEADS, HEAD_DIM = 8, 32
FF = 512
FILTERS, RADIAL = 128, 32
EDGE_DIM = 128
NB = -(-N_NODES // P)
N_PAD = NB * P
LAST = N_NODES - (NB - 1) * P
TILES = -(-N_EDGES // P)
GROUPS = -(-TILES // P)
E_PAD = GROUPS * P * P
G = 8
RING = 4
BATCHES = -(-(TILES + NB - 1) // G)
TURNS = BATCHES // RING
STEPS = (BATCHES + 4) * G
HALF = STEPS // 2
SLOTS = G * P
NO_NODE = 1 << 24
BIG = 1e30
ROWS_OUT = 4
LN_EPS = BN_EPS = 1e-5
ATT0_SLOPE, ATT2_SLOPE = 0.2, 0.01
CUTOFF = 5.0
ROUNDER = 1.5 * 2.0 ** 23
ROW0 = D + HEADS
ACC_W = D + 2 * HEADS + 1
ROW2 = D + 2
CHUNK = 448
CHUNKS = N_PAD // CHUNK

CONST = {}
_at = 0
for _name, _w in (("iota_k", STEPS), ("iota_n", P), ("ident", P), ("tile", GROUPS), ("p_first", 1), ("p_last", 1)):
    CONST[_name] = (_at, _at + _w)
    _at += _w
CONST_W = _at

COLS = {}
_at = 0
for _name, _w in (("bo", 2), ("bn1_g", 2), ("bn1_b", 2), ("b1", 4), ("b2", 2), ("bn2_g", 2), ("bn2_b", 2),
                  ("b_n2m", 1), ("b_lin2", 1), ("be", 2), ("attn", 2)):
    COLS[_name] = (_at, _at + _w)
    _at += _w
COLS_W = _at


def ready(b):
    return b + 3


def free(b):
    return b + 1


def later(n, than=0):
    return not isinstance(n, int) or n > than


def each(turn, eng, count, body, peeled=0):
    for b in range(peeled):
        body(b, b % turn, True)
    with eng.Fori(peeled // turn, (count - 1) // turn) as i:
        for u in range(turn):
            body(turn * i + u, u, True)
    for b in range((count - 1) // turn * turn, count):
        body(b, b % turn, b < count - 1)


def each_pair(eng, count, body, peeled=0):
    each(2, eng, count, body, peeled)


def build(nc, inp, out):
    top = ExitStack()
    with top:
        carriers = nc.alloc_semaphore("carriers")
        held = []

        def sem(name):
            held.append(nc.alloc_semaphore(name))
            return held[-1]

        def layer_ends():
            nc.clear_and_free_semaphores(held)
            held.clear()
            nc.all_engine_barrier()

        def sb(stack, name, shape, dt=F32):
            return stack.enter_context(nc.sbuf_tensor(name, shape, dt))

        def scratch(name, shape, dt=F32):
            return nc.dram_tensor(name, shape, dt, kind="Internal").ap()

        table0 = scratch("table0", (N_PAD, ROW0))
        table1 = scratch("table1", (N_PAD, FILTERS))
        table2 = scratch("table2", (N_PAD, ROW2))
        table3 = scratch("table3", (N_PAD, D))
        key_line = scratch("key_line", (1 + GROUPS * P * P,))
        restart_line = scratch("restart_line", (GROUPS * P * P + 1,), BF16)

        banks = top.enter_context(nc.psum_tensor("banks", [P, 8, 512], F32))

        const = sb(top, "const", [P, CONST_W])
        cols = sb(top, "cols", [P, COLS_W])
        X = sb(top, "X", [P, NB, D])
        acc = sb(top, "acc", [P, NB, ACC_W])
        src_idx = sb(top, "src_idx", [P, STEPS], I32)
        dst_loc = sb(top, "dst_loc", [P, STEPS])
        cutoff = sb(top, "cutoff", [P, STEPS])
        edge_q = sb(top, "edge_q", [P, STEPS])
        step_block = sb(top, "step_block", [1, STEPS], I32)
        step_tile = sb(top, "step_tile", [1, STEPS], I32)
        same_first = sb(top, "same_first", [P, BATCHES + 1])
        same_last = sb(top, "same_last", [P, BATCHES + 1])
        stats = sb(top, "stats", [P, NB, 6])
        rstd = sb(top, "rstd", [P, NB])
        nbias = sb(top, "nbias", [P, NB])
        degree = sb(top, "degree", [P, NB])
        dinv = sb(top, "dinv", [P, NB])
        gcn_bias = sb(top, "gcn_bias", [P, D])
        eps = sb(top, "eps", [P, 1])
        ones = sb(top, "ones", [P, P])
        scores = sb(top, "scores", [P, NB, HEADS])

        def const_(name):
            return const[:, CONST[name][0]:CONST[name][1]]

        def col(name, f=0):
            return cols[:, COLS[name][0] + f:COLS[name][0] + f + 1]

        ident = const_("ident")
        iota_n = const_("iota_n")

        def node_rows(ap, b):
            return ap[bass.ds(b * P, P), :]

        st = ExitStack()
        with st:
            dst_i = sb(st, "dst_i", [P, GROUPS, P], I32)
            src_i = sb(st, "src_i", [P, GROUPS, P], I32)
            next_i = sb(st, "next_i", [P, GROUPS, 1], I32)
            block_i = sb(st, "block_i", [P, 2, GROUPS], I32)
            dst_f = sb(st, "dst_f", [P, GROUPS, P])
            src_f = sb(st, "src_f", [P, GROUPS, P])
            wgt = sb(st, "wgt", [P, GROUPS, P])
            turn = sb(st, "turn", [P, GROUPS, P])
            first_step = sb(st, "first_step", [P, 2, GROUPS])
            work = acc[:, :, :].rearrange("p b w -> p (b w)")[:, 0:2 * GROUPS * STEPS].rearrange("p (o g k) -> p o g k", o=2, g=GROUPS)
            begun, pick = work[:, 0, :, :], work[:, 1, :, :]
            block = sb(st, "block", [P, STEPS])
            valid = sb(st, "valid", [P, 2, STEPS])
            key = sb(st, "key", [P, GROUPS * P])
            key_row = sb(st, "key_row", [P, GROUPS, P])
            key_prev = sb(st, "key_prev", [P, GROUPS, P])
            differ = sb(st, "differ", [P, GROUPS, P])
            restart = sb(st, "restart", [P, GROUPS, P], BF16)
            mark = sb(st, "mark", [1, 1])
            mark_b = sb(st, "mark_b", [1, 1], BF16)
            goes_on_b = sb(st, "goes_on_b", [1, BATCHES + 1], BF16)
            goes_on = sb(st, "goes_on", [1, BATCHES + 1])

            const_in, dst_in, src_in, next_in, wgt_in, x_in, bias_in = (sem(n) for n in (
                "const_in", "dst_in", "src_in", "next_in", "wgt_in", "x_in", "bias_in"))
            idx_dve = sem("idx_dve")
            sine_done = sem("sine_done")
            picked = sem("picked")
            key_turned = sem("key_turned")
            key_rows = sem("key_rows")
            key_out, key_back, restart_out, goes_on_in = (sem(n) for n in (
                "key_out", "key_back", "restart_out", "goes_on_in"))
            goes_on_ready, goes_on_spread = sem("goes_on_ready"), sem("goes_on_spread")
            restart_ready = sem("restart_ready")

            with nc.Block() as blk:
                at = {}

                @blk.vector
                def _(dve):
                    def step(ins, name=""):
                        at["last"] = at.get("last", 0) + 1
                        at[name] = at["last"]
                        ins.then_inc(idx_dve, 1)
                        return at["last"]

                    v = nc.vector
                    v.memset(eps[:, :], LN_EPS)
                    v.memset(ones[:, :], 1.0)
                    v.memset(mark[:, :], -1.0)
                    v.memset(mark_b[:, :], -BIG)
                    step(v.memset(key[:, :], 0.0))
                    dve.wait_ge(dst_in, 16)
                    dve.wait_ge(next_in, 16)
                    v.tensor_scalar(block_i[:, 0, :].unsqueeze(2), dst_i[:, :, 0:1], 7, None, ALU.arith_shift_right)
                    v.tensor_scalar(block_i[:, 1, :].unsqueeze(2), next_i[:, :, :], 7, None, ALU.arith_shift_right)
                    dve.wait_ge(const_in, 32)
                    now = step(v.tensor_copy(dst_f[:, :, :], dst_i[:, :, :]))
                    dve.wait_ge(idx_dve, now)
                    v.tensor_tensor(first_step[:, 0, :], block_i[:, 0, :], const_("tile"), ALU.add)
                    now = step(v.scalar_tensor_tensor(first_step[:, 1, :], block_i[:, 1, :], 1.0, const_("tile"), ALU.add, ALU.add))
                    dve.wait_ge(src_in, 16)
                    now = step(v.tensor_copy(src_f[:, :, :], src_i[:, :, :]))
                    dve.wait_ge(idx_dve, now)
                    for g in range(GROUPS):
                        last = v.tensor_scalar(begun[:, g, :], const_("iota_k"), first_step[:, 0, g:g + 1], None, ALU.is_ge)
                    now = step(last)
                    dve.wait_ge(idx_dve, now)
                    for g in range(GROUPS):
                        last = v.scalar_tensor_tensor(pick[:, g, :], const_("iota_k"), first_step[:, 1, g:g + 1], begun[:, g, :], ALU.is_lt, ALU.mult)
                    dve.wait_ge(wgt_in, 16)
                    now = step(v.tensor_scalar(turn[:, :, :], wgt[:, :, :], 0.5 / CUTOFF, None, ALU.mult), "pick")
                    dve.wait_ge(idx_dve, now)
                    now = step(v.tensor_scalar(wgt[:, :, :], turn[:, :, :], ROUNDER, None, ALU.add))
                    dve.wait_ge(idx_dve, now)
                    now = step(v.tensor_scalar(wgt[:, :, :], wgt[:, :, :], ROUNDER, None, ALU.subtract))
                    dve.wait_ge(idx_dve, now)
                    step(v.tensor_tensor(turn[:, :, :], turn[:, :, :], wgt[:, :, :], ALU.subtract), "turn")
                    dve.wait_ge(sine_done, 1)
                    now = step(v.tensor_tensor(turn[:, :, :], wgt[:, :, :], wgt[:, :, :], ALU.mult))
                    dve.wait_ge(idx_dve, now)
                    step(v.tensor_scalar(turn[:, :, :], turn[:, :, :], -1.0, 1.0, ALU.mult, ALU.add), "cutoff")
                    def row_stats_of(first, end):
                        with dve.Fori(first // 4, end // 4) as i:
                            for r in range(4):
                                b = 4 * i + r
                                v.bn_stats(stats[:, bass.ds(b, 1), :].squeeze(1), X[:, bass.ds(b, 1), :].squeeze(1))

                    def halves(tile):
                        return tile[:, :].rearrange("p (h k) -> p h k", h=2)

                    dve.wait_ge(picked, 1)
                    iota_k2 = const_("iota_k").rearrange("p (h k) -> p h k", h=2)
                    now = step(v.scalar_tensor_tensor(halves(block), iota_k2, 1.0, banks[:, 0:2, 0:HALF], ALU.add, ALU.subtract))
                    v.tensor_scalar(step_tile[:, :].rearrange("p (h k) -> p h k", h=2), banks[0:1, 0:2, 0:HALF], 1.0, 0.0, ALU.subtract, ALU.max)
                    dve.wait_ge(idx_dve, now)
                    v.tensor_scalar(step_block[:, :], block[0:1, :], float(NB - 1), None, ALU.min)
                    dve.wait_ge(x_in, 16)
                    row_stats_of(0, 16)
                    dve.wait_ge(picked, 2)
                    now = step(v.scalar_tensor_tensor(halves(dst_loc), halves(block), -float(P), banks[:, 2:4, 0:HALF], ALU.mult, ALU.add))
                    dve.wait_ge(idx_dve, now)
                    now = step(v.tensor_scalar(valid[:, 0, :], dst_loc[:, :], 0.0, None, ALU.is_ge))
                    dve.wait_ge(idx_dve, now)
                    now = step(v.scalar_tensor_tensor(valid[:, 1, :], dst_loc[:, :], float(P), valid[:, 0, :], ALU.is_lt, ALU.mult))
                    dve.wait_ge(idx_dve, now)
                    step(v.scalar_tensor_tensor(halves(key[:, 0:STEPS]), banks[:, 2:4, 0:HALF], 1.0, halves(valid[:, 1, :]), ALU.add, ALU.mult), "key")
                    row_stats_of(16, 32)
                    dve.wait_ge(picked, 3)
                    v.tensor_copy(halves(src_idx), banks[:, 4:6, 0:HALF])
                    dve.wait_ge(key_turned, 1)
                    v.tensor_copy(key_row[:, 0:4, :], banks[:, 0, :].rearrange("p (g e) -> p g e", g=4)).then_inc(key_rows, 1)
                    v.tensor_copy(key_row[:, 4:GROUPS, :], banks[:, 1, 0:(GROUPS - 4) * P].rearrange("p (g e) -> p g e", g=GROUPS - 4)).then_inc(key_rows, 1)
                    row_stats_of(32, NB // 4 * 4)
                    for b in range(NB // 4 * 4, NB):
                        v.bn_stats(stats[:, b, :], X[:, b, :])
                    dve.wait_ge(key_rows, 2)
                    dve.wait_ge(key_back, 16)
                    now = step(v.tensor_tensor(differ[:, :, :], key_row[:, :, :], key_prev[:, :, :], ALU.not_equal))
                    dve.wait_ge(idx_dve, now)
                    v.tensor_scalar(restart[:, :, :], differ[:, :, :], -BIG, None, ALU.mult).then_inc(restart_ready, 1)
                    dve.wait_ge(picked, 4)
                    v.tensor_copy(halves(cutoff), banks[:, 6:8, 0:HALF])
                    dve.wait_ge(goes_on_in, 16)
                    v.tensor_scalar(goes_on[:, :], goes_on_b[:, :], 0.0, None, ALU.is_equal).then_inc(goes_on_ready, 1)
                    dve.wait_ge(goes_on_spread, 1)
                    v.tensor_scalar(same_first[:, :], banks[:, 2, 0:BATCHES + 1], const_("p_first"), None, ALU.mult)
                    v.tensor_scalar(same_last[:, :], banks[:, 2, 0:BATCHES + 1], const_("p_last"), None, ALU.mult)

                @blk.sync
                def _(sp):
                    sp.dma_start(const[:, :], inp["const"]).then_inc(const_in, 16)
                    sp.dma_start(dst_i[:, :, :], inp["dst"][0:E_PAD].rearrange("(g p e) -> p g e", p=P, e=P)).then_inc(dst_in, 16)
                    with nc.allow_non_contiguous_dma(reason="one word of each tile"):
                        sp.dma_start(next_i[:, :, :], inp["dst"][P:P + E_PAD].rearrange("(g p e) -> p g e", p=P, e=P)[:, :, 0:1]).then_inc(next_in, 16)
                    sp.dma_start(src_i[:, :, :], inp["src"].rearrange("(g p e) -> p g e", p=P, e=P)).then_inc(src_in, 16)
                    sp.dma_start(wgt[:, :, :], inp["edge_weight"].rearrange("(g p e) -> p g e", p=P, e=P)).then_inc(wgt_in, 16)
                    sp.dma_start(cols[:, :], inp["cols"]).then_inc(const_in, 16)
                    sp.dma_start(gcn_bias[:, :], inp["b3"].partition_broadcast(P)).then_inc(bias_in, 16)
                    sp.dma_start(X[:, :, :], inp["x"].rearrange("(b p) d -> p b d", p=P)).then_inc(x_in, 16)
                    sp.wait_ge(key_rows, 2)
                    sp.dma_start(key_line[1:1 + GROUPS * P * P].rearrange("(g p e) -> p g e", p=P, e=P), key_row[:, :, :]).then_inc(key_out, 16)
                    sp.dma_start(key_line[0:1].unsqueeze(0), mark[:, :]).then_inc(key_out, 16)
                    sp.wait_ge(key_out, 32)
                    sp.dma_start(key_prev[:, :, :], key_line[0:GROUPS * P * P].rearrange("(g p e) -> p g e", p=P, e=P)).then_inc(key_back, 16)
                    sp.wait_ge(restart_ready, 1)
                    sp.dma_start(restart_line[0:GROUPS * P * P].rearrange("(g p e) -> p g e", p=P, e=P), restart[:, :, :]).then_inc(restart_out, 16)
                    sp.dma_start(restart_line[GROUPS * P * P:].unsqueeze(0), mark_b[:, :]).then_inc(restart_out, 16)
                    sp.wait_ge(restart_out, 32)
                    with nc.allow_non_contiguous_dma(reason="one word of each batch"):
                        sp.dma_start(goes_on_b[:, :].unsqueeze(2), restart_line[0:(BATCHES + 1) * SLOTS].rearrange("(o j e) -> o j e", o=1, e=SLOTS)[:, :, 0:1]).then_inc(goes_on_in, 16)
                    sp.wait_ge(x_in, 16)
                    sp.wait_ge(bias_in, 16)

                @blk.scalar
                def _(act):
                    act.wait_ge(idx_dve, at["turn"])
                    nc.scalar.activation(wgt[:, :, :], turn[:, :, :], ACT.Sin, scale=float(np.pi)).then_inc(sine_done, 1)

                @blk.tensor
                def _(pe):
                    def pick_rows(bank, rows, by):
                        for h in range(2):
                            for g in range(GROUPS):
                                last = nc.tensor.matmul(banks[:, bank + h, 0:HALF], rows(g), by[:, g, h * HALF:(h + 1) * HALF],
                                                        start=(g == 0), stop=(g == GROUPS - 1))
                        last.then_inc(picked, 1)

                    pe.wait_ge(idx_dve, at["pick"])
                    pick_rows(0, lambda g: ones[:, :], begun)
                    pick_rows(2, lambda g: dst_f[:, g, :], pick)
                    pick_rows(4, lambda g: src_f[:, g, :], pick)
                    pe.wait_ge(idx_dve, at["key"])
                    for g in range(GROUPS):
                        last = nc.tensor.transpose(banks[:, g // 4, (g % 4) * P:(g % 4 + 1) * P], key[:, g * P:(g + 1) * P], ident)
                    last.then_inc(key_turned, 1)
                    pe.wait_ge(idx_dve, at["cutoff"])
                    pick_rows(6, lambda g: turn[:, g, :], pick)
                    pe.wait_ge(goes_on_ready, 1)
                    nc.tensor.matmul(banks[:, 2, 0:BATCHES + 1], ones[0:1, :], goes_on[:, :], start=True, stop=True).then_inc(goes_on_spread, 1)

        def norm_coefs(dve, name, work, root_ready, steps):
            v = nc.vector
            mean, diff, var = work[:, 0, :], work[:, 1, :], work[:, 2, :]
            even_mean, even_m2, odd_mean, odd_m2 = (stats[:, :, i] for i in (1, 2, 4, 5))
            n = 0

            def link(ins):
                nonlocal n
                n += 1
                ins.then_inc(steps, 1)
                dve.wait_ge(steps, n)

            v.tensor_tensor(mean, even_mean, odd_mean, ALU.add)
            v.tensor_tensor(diff, even_mean, odd_mean, ALU.subtract)
            link(v.tensor_tensor(var, even_m2, odd_m2, ALU.add))
            v.tensor_scalar(mean, mean, 0.5, None, ALU.mult)
            link(v.scalar_tensor_tensor(diff, diff, 0.25, diff, ALU.mult, ALU.mult))
            link(v.scalar_tensor_tensor(var, var, 1.0 / D, diff, ALU.mult, ALU.add))
            dve.wait_ge(root_ready, 1)
            link(v.reciprocal(rstd[:, :], work[:, 3, :]))
            link(v.scalar_tensor_tensor(nbias[:, :], mean, -1.0, rstd[:, :], ALU.mult, ALU.mult))

        VAR_STEP, COEF_STEP = 3, 5

        def node_stage(tag, weights, weight_cols, load_extra, pe_mm, pe_mm2, dve_row, act_mid, pool_extra, table, row_w, row_init, extra_alloc):
            st = ExitStack()
            with st:
                w = sb(st, f"{tag}_w", [P, weight_cols])
                work = sb(st, f"{tag}_work", [P, 4, NB])
                h = sb(st, f"{tag}_h", [P, 2, D])
                hT = sb(st, f"{tag}_hT", [P, 2, 2, P])
                row = sb(st, f"{tag}_row", [P, ROWS_OUT, row_w])
                extra = extra_alloc(st) if extra_alloc else None
                w_in, extra_in = sem(f"{tag}_w_in"), sem(f"{tag}_extra_in") if load_extra else None
                steps, root_ready = sem(f"{tag}_coef_steps"), sem(f"{tag}_root")
                h_ready, turned, hT_ready, product, row_ready = (sem(f"{tag}_{n}") for n in (
                    "h_ready", "turned", "hT_ready", "product", "row_ready"))
                mid_product, mid_ready = (sem(f"{tag}_mid_product"), sem(f"{tag}_mid_ready")) if act_mid else (None, None)
                row_taken = sem(f"{tag}_row_taken") if pool_extra else None
                row_free = [sem(f"{tag}_stored{u}") for u in range(ROWS_OUT)]
                chain = sem(f"{tag}_chain") if load_extra else None
                S = dict(w=w, h=h, hT=hT, row=row, extra=extra, product=product, row_ready=row_ready, chain=chain, mid_product=mid_product,
                         mid_ready=mid_ready, hT_ready=hT_ready, row_taken=row_taken)

                with nc.Block() as blk:
                    @blk.sync
                    def _(sp):
                        sp.dma_start(w[:, :], weights).then_inc(w_in, 16)
                        if load_extra:
                            load_extra(sp, extra, extra_in)

                        def store(b, u, _):
                            sp.wait_ge(row_ready, ready(b))
                            sp.sem_inc(carriers, 1)
                            sp.dma_start(node_rows(table, b), row[:, u, :]).then_inc(row_free[u], 16)

                        each(ROWS_OUT, sp, NB, store)
                        for u in range(ROWS_OUT):
                            sp.wait_ge(row_free[u], 16 * ((NB - 1 - u) // ROWS_OUT + 1))

                    @blk.gpsimd
                    def _(pool):
                        if tag != "n3":
                            nc.gpsimd.memset(acc[:, :, :], 0.0)
                        if pool_extra:
                            pool.sem_inc(row_taken, 2)
                            each(ROWS_OUT, pool, NB, lambda b, u, _: pool_extra(pool, b, u, S))

                    @blk.scalar
                    def _(act):
                        act.sem_inc(h_ready, 2)
                        act.sem_inc(hT_ready, 2)
                        if act_mid:
                            act.sem_inc(mid_ready, 2)
                        act.wait_ge(steps, VAR_STEP)
                        nc.scalar.activation(work[:, 3, :], work[:, 2, :], ACT.Sqrt, bias=eps[:, 0:1]).then_inc(root_ready, 1)
                        act.wait_ge(steps, COEF_STEP)

                        def normed(b, u):
                            act.wait_ge(turned, free(b))
                            nc.scalar.activation(h[:, u, :], X[:, bass.ds(b, 1), :].squeeze(1), ACT.Relu,
                                                 bias=nbias[:, bass.ds(b, 1)], scale=rstd[:, bass.ds(b, 1)]).then_inc(h_ready, 1)

                        def block(b, u, more):
                            if more:
                                normed(b + 1, 1 - u)
                            act.wait_ge(turned, ready(b))
                            act.wait_ge(mid_product if act_mid else product, free(b))
                            nc.scalar.copy(hT[:, u, :, :], banks[:, u, 0:D].rearrange("p (f n) -> p f n", f=2)).then_inc(hT_ready, 1)
                            if act_mid and (later(b)):
                                act_mid(act, b - 1, 1 - u, S)

                        normed(0, 0)
                        each_pair(act, NB, block, 2)
                        if act_mid:
                            act_mid(act, NB - 1, (NB - 1) % 2, S)

                    @blk.tensor
                    def _(pe):
                        pe.sem_inc(turned, 2)
                        pe.sem_inc(product, 2)
                        if act_mid:
                            pe.sem_inc(mid_product, 2)
                        pe.wait_ge(w_in, 16)

                        def turn(b, u):
                            pe.wait_ge(h_ready, ready(b))
                            pe.wait_ge(hT_ready, free(b))
                            for f in range(2):
                                last = nc.tensor.transpose(banks[:, u, f * P:(f + 1) * P], h[:, u, f * P:(f + 1) * P], ident)
                            last.then_inc(turned, 1)

                        def block(b, u, more):
                            if more:
                                turn(b + 1, 1 - u)
                            pe.wait_ge(hT_ready, ready(b))
                            pe_mm(pe, b, u, S)
                            if pe_mm2 and (later(b)):
                                pe_mm2(pe, b - 1, 1 - u, S)

                        turn(0, 0)
                        each_pair(pe, NB, block, 2)
                        if pe_mm2:
                            pe_mm2(pe, NB - 1, (NB - 1) % 2, S)

                    @blk.vector
                    def _(dve):
                        dve.sem_inc(row_ready, 2)
                        norm_coefs(dve, tag, work, root_ready, steps)
                        for c, value in row_init:
                            nc.vector.memset(row[:, :, c:c + 1], value)
                        if load_extra:
                            dve.wait_ge(extra_in, 16)

                        def block(b, u, _):
                            dve.wait_ge(product, ready(b))
                            if later(b, ROWS_OUT - 1):
                                dve.wait_ge(row_free[u], (b - u) * (16 // ROWS_OUT))
                                if pool_extra:
                                    dve.wait_ge(row_taken, ready(b - ROWS_OUT))
                            dve_row(dve, b, u, S)

                        each(ROWS_OUT, dve, NB, block, ROWS_OUT)

        def qkv_mm(pe, b, u, S):
            pe.wait_ge(S["row_ready"], free(b))
            w, hT = S["w"], S["hT"]
            for bank, c0, c1 in ((2 + 2 * u, 0, 2 * D), (3 + 2 * u, 2 * D, 3 * D)):
                for k in range(2):
                    last = nc.tensor.matmul(banks[:, bank, 0:c1 - c0], hT[:, u, k, :], w[:, 3 * D * k + c0:3 * D * k + c1],
                                            start=(k == 0), stop=(k == 1))
            last.then_inc(S["product"], 1)

        def qkv_row(dve, b, u, S):
            bias, qk = S["extra"]
            row, chain = S["row"], S["chain"]
            v = nc.vector
            w = u % 2
            v.tensor_tensor(qk[:, w, :], banks[:, 2 + 2 * w, 0:2 * D], bias[:, 0:2 * D], ALU.add).then_inc(chain, 1)
            v.tensor_tensor(row[:, u, 0:D], banks[:, 3 + 2 * w, 0:D], bias[:, 2 * D:3 * D], ALU.add)
            dve.wait_ge(chain, 2 * b + 1)
            v.scalar_tensor_tensor(qk[:, w, 0:D], qk[:, w, 0:D], float(HEAD_DIM) ** -0.5, qk[:, w, D:2 * D], ALU.mult, ALU.mult).then_inc(chain, 1)
            dve.wait_ge(chain, 2 * b + 2)
            v.tensor_reduce(row[:, u, D:ROW0], qk[:, w, 0:D].rearrange("p (h c) -> p h c", h=HEADS), AX_X, ALU.add).then_inc(S["row_ready"], 1)

        def keep_scores(pool, b, u, S):
            pool.wait_ge(S["row_ready"], ready(b))
            nc.gpsimd.tensor_copy(scores[:, bass.ds(b, 1), :].squeeze(1), S["row"][:, u, D:ROW0]).then_inc(S["row_taken"], 1)

        def qkv_alloc(st):
            return sb(st, "qkv_bias", [P, 3 * D]), sb(st, "qk", [P, 2, 2 * D])

        def qkv_load(sp, extra, done):
            sp.dma_start(extra[0][:, :], inp["bqkv"].partition_broadcast(P)).then_inc(done, 16)

        def filter_alloc(st):
            return sb(st, "mid", [P, 2, P])

        def filter_mm(pe, b, u, S):
            w, hT = S["w"], S["hT"]
            pe.wait_ge(S["mid_ready"], free(b))
            for k in range(2):
                last = nc.tensor.matmul(banks[:, 2 + u, 0:P], w[:, k * FILTERS:(k + 1) * FILTERS], hT[:, u, k, :], start=(k == 0), stop=(k == 1))
            last.then_inc(S["mid_product"], 1)

        def filter_mm2(pe, b, u, S):
            pe.wait_ge(S["mid_ready"], ready(b))
            pe.wait_ge(S["row_ready"], free(b))
            nc.tensor.matmul(banks[:, 4 + u, 0:FILTERS], S["extra"][:, u, :], S["w"][:, 2 * FILTERS:3 * FILTERS], start=True, stop=True).then_inc(S["product"], 1)

        def filter_mid(act, b, u, S):
            act.wait_ge(S["mid_product"], ready(b))
            act.wait_ge(S["product"], free(b))
            nc.scalar.activation(S["extra"][:, u, :], banks[:, 2 + u, 0:P], ACT.Identity, bias=col("b_n2m")).then_inc(S["mid_ready"], 1)

        def filter_row(dve, b, u, S):
            nc.vector.tensor_copy(S["row"][:, u, :], banks[:, 4 + u % 2, 0:FILTERS]).then_inc(S["row_ready"], 1)

        def wn_alloc(st):
            return sb(st, "wn_rows", [P, 2 * D]), sb(st, "wn_junk", [P, 2, D])

        def wn_load(sp, extra, done):
            sp.dma_start(extra[0][:, :], inp["bn_attn"].partition_broadcast(P)).then_inc(done, 16)

        def wn_mm(pe, b, u, S):
            pe.wait_ge(S["row_ready"], free(b))
            for k in range(2):
                last = nc.tensor.matmul(banks[:, 2 + u, 0:D], S["hT"][:, u, k, :], S["w"][:, k * D:(k + 1) * D], start=(k == 0), stop=(k == 1))
            last.then_inc(S["product"], 1)

        def wn_row(dve, b, u, S):
            vectors, junk = S["extra"]
            row, chain = S["row"], S["chain"]
            nc.vector.tensor_tensor(row[:, u, 0:D], banks[:, 2 + u % 2, 0:D], vectors[:, 0:D], ALU.add).then_inc(chain, 1)
            dve.wait_ge(chain, b + 1)
            nc.vector.scalar_tensor_tensor(junk[:, u % 2, :], row[:, u, 0:D], 1.0, vectors[:, D:2 * D], ALU.mult, ALU.mult,
                                           accum_out=row[:, u, D + 1:D + 2]).then_inc(S["row_ready"], 1)

        gcn_mm = wn_mm

        def gcn_row(dve, b, u, S):
            nc.vector.tensor_scalar(S["row"][:, u, :], banks[:, 2 + u % 2, 0:D], dinv[:, bass.ds(b, 1)], None, ALU.mult).then_inc(S["row_ready"], 1)

        def keep_own(pool, b, u, S):
            pool.wait_ge(S["row_ready"], ready(b))
            nc.gpsimd.tensor_copy(acc[:, bass.ds(b, 1), 0:D].squeeze(1), S["row"][:, u, :]).then_inc(S["row_taken"], 1)

        def gather_batches(pool, table, width, rows, stage, staged, gathered, summed_tile, ahead):
            def gather(n, u):
                pool.wait_ge(summed_tile, summed(n - RING, G - 1))
                pool.sem_inc(carriers, 1)
                pool.wait_ge(staged, n + 1)
                pool.sem_inc(carriers, 1)
                for q in range(G):
                    nc.gpsimd.indirect_dma_start(out=rows[:, u, q, 0:width], out_offset=None, in_=table,
                                                 in_offset=bass.IndirectOffsetOnAxis(ap=stage[:, u, q:q + 1], axis=0)).then_inc(gathered[u], 16)

            for n in range(ahead):
                gather(n, n)
            with pool.Fori(0, TURNS) as i:
                for r in range(RING):
                    gather(i * RING + r + ahead, (r + ahead) % RING)
            for u in range(RING):
                pool.wait_ge(gathered[u], 16 * G * (TURNS + (u < ahead)))

        def stage_indices(act, n, u, stage, staged, gathered):
            if later(n, RING - 1):
                act.wait_ge(gathered[u], arrived(n - RING, u))
            nc.scalar.copy(stage[:, u, :], src_idx[:, bass.ds(n * G, G)]).then_inc(staged, 1)

        def arrived(n, u):
            return (n - u) * (16 * G // RING) + 16 * G

        def load_blocks(engine, n):
            return nc.values_load_multi_w_load_instructions(
                step_block[0:1, bass.ds(n * G, G)], engines=[engine], min_val=0, max_val=NB - 1,
                skip_runtime_bounds_check_because="clamped when they were made")[1]

        def summed(j, q):
            return (j + RING) * G + q + 1

        def sum_tile(pe, j, q, onehot, rows, summed_tile, added, width):
            pe.wait_ge(added, j * G + q + 1)
            nc.tensor.matmul(banks[:, 2 + q % 4, 0:width], onehot, rows, start=True, stop=True).then_inc(summed_tile, 1)

        def add_tile(dve, j, q, block, summed_tile, added, width):
            dve.wait_ge(summed_tile, summed(j, q))
            dve.wait_ge(added, j * G + q + 4)
            at = acc[:, bass.ds(block, 1), 0:width].squeeze(1)
            nc.vector.tensor_tensor(at, at, banks[:, 2 + q % 4, 0:width], ALU.add).then_inc(added, 1)

        def softmax_edges(tag, table, row_w, sum_w, heads):
            many = heads > 1
            slope = ATT0_SLOPE if many else ATT2_SLOPE
            GH = G * heads
            ring_w = max(row_w, sum_w)
            st = ExitStack()
            with st:
                rows = sb(st, f"{tag}_rows", [P, RING, G, ring_w])
                stage = sb(st, f"{tag}_stage", [P, RING, G], I32)
                hot = sb(st, f"{tag}_hot", [P, RING, G, P])
                apart = sb(st, f"{tag}_apart", [P, G, P])
                restart = sb(st, f"{tag}_restart", [heads, 2, SLOTS + 1], BF16)
                maxes = sb(st, f"{tag}_maxes", [heads, SLOTS])
                val = sb(st, f"{tag}_val", [P, GH])
                sums = sb(st, f"{tag}_sums", [P, 3, GH])
                leaky = sb(st, f"{tag}_leaky", [P, RING, 3, GH])
                power = sb(st, f"{tag}_power", [P, 2, GH])
                scale_to = sb(st, f"{tag}_scale_to", [P, heads])
                ends = sb(st, f"{tag}_ends", [P, RING, 2, heads])
                if many:
                    hotT = sb(st, f"{tag}_hotT", [P, G, P])
                    at_dst = sb(st, f"{tag}_at_dst", [P, GH])
                else:
                    weight = sb(st, f"{tag}_weight", [P, RING, G])
                    weighted_hot = sb(st, f"{tag}_weighted_hot", [P, 2, G, P])
                gathered = [sem(f"{tag}_gathered{u}") for u in range(RING)]
                restart_in = [sem(f"{tag}_restart_in{u}") for u in range(2)]
                (staged, apart_ready, hot_ready, val_ready, val_turned, scan_fwd, scan_ready, max_turned, leaky_ready, power_ready, ends_ready, exp_ready,
                 weighted, delta_ready, scale_ready, scaled, summed_tile, added, logit_ready) = (sem(f"{tag}_{n}") for n in (
                     "staged", "apart_ready", "hot_ready", "val_ready", "val_turned", "scan_fwd", "scan_ready", "max_turned", "leaky_ready",
                     "power_ready", "ends_ready", "exp_ready", "weighted", "delta_ready", "scale_ready", "scaled", "summed_tile", "added", "logit_ready"))
                if many:
                    hotT_psum, hotT_ready, dst_scores, sums_ready, own_ready = (sem(f"{tag}_{n}") for n in (
                        "hotT_psum", "hotT_ready", "dst_scores", "sums_ready", "own_ready"))
                scan_psum = banks[0:heads, 0:2, :].rearrange("h b e -> h (b e)")
                DST_AT, MAX_AT = 0, 128

                with nc.Block() as blk:
                    @blk.gpsimd
                    def _(pool):
                        gather_batches(pool, table, row_w, rows, stage, staged, gathered, summed_tile, 2)

                    @blk.sync
                    def _(sp):
                        def load(n, u):
                            sp.wait_ge(scan_ready, free(n))
                            sp.sem_inc(carriers, 1)
                            sp.dma_start(restart[:, u, :], restart_line[bass.ds(n * SLOTS, SLOTS + 1)].partition_broadcast(heads)).then_inc(restart_in[u], 16)

                        load(0, 0)
                        with sp.Fori(0, BATCHES // 2) as i:
                            load(2 * i + 1, 1)
                            load(2 * i + 2, 0)
                        sp.wait_ge(restart_in[0], 16 * (BATCHES // 2 + 1))
                        sp.wait_ge(restart_in[1], 16 * (BATCHES // 2))

                    @blk.scalar
                    def _(act):
                        def one_hot(n, u):
                            if later(n):
                                act.wait_ge(hot_ready, n)
                            for q in range(G):
                                last = nc.scalar.activation(apart[:, q, :], iota_n, ACT.Abs, bias=dst_loc[:, bass.ds(n * G + q, 1)], scale=-1.0)
                            last.then_inc(apart_ready, 1)
                            act.wait_ge(apart_ready, n + 1)
                            nc.scalar.activation(hot[:, u, :, :], apart[:, :, :], ACT.Relu, bias=ones[:, 0:1], scale=-1.0).then_inc(hot_ready, 1)

                        def keep_hotT(n):
                            for g in range(G // 4):
                                act.wait_ge(hotT_psum, n * (G // 4) + g + 1)
                                if later(n):
                                    act.wait_ge(dst_scores, n)
                                nc.scalar.copy(hotT[:, 4 * g:4 * g + 4, :], banks[:, 6, :].rearrange("p (q e) -> p q e", q=4)).then_inc(hotT_ready, 1)

                        def own_logit(n):
                            act.wait_ge(logit_ready, n + 1)
                            act.wait_ge(leaky_ready, n + 1)
                            nc.scalar.activation(sums[:, 1, :], at_dst[:, :], ACT.Copy, scale=2.0).then_inc(own_ready, 1)

                        def exponent(n, u):
                            act.wait_ge(power_ready, n + 1)
                            if many:
                                to = rows[:, u, :, D:D + 2 * HEADS].rearrange("p t (c h) -> p c t h", c=2)
                                nc.scalar.activation(to, power[:, :, :].rearrange("p c (t h) -> p c t h", t=G), ACT.Exp).then_inc(exp_ready, 1)
                            else:
                                nc.scalar.activation(weight[:, u, :], power[:, 0, :], ACT.Exp).then_inc(exp_ready, 1)
                                act.wait_ge(hot_ready, n + 1)
                                act.wait_ge(exp_ready, n + 1)
                                act.wait_ge(summed_tile, summed(n - 2, G - 1))
                                for q in range(G):
                                    nc.scalar.activation(weighted_hot[:, u % 2, q, :], hot[:, u, q, :], ACT.Copy, scale=weight[:, u, q:q + 1]).then_inc(weighted, 1)
                            if many:
                                act.wait_ge(leaky_ready, n + 2)
                                nc.scalar.activation(ends[:, u, 0, :], leaky[:, u, 2, 0:heads], ACT.Copy, scale=same_first[:, bass.ds(n, 1)])
                                nc.scalar.activation(ends[:, u, 1, :], leaky[:, (u - 1) % RING, 2, GH - heads:GH], ACT.Copy,
                                                     scale=same_last[:, bass.ds(n, 1)]).then_inc(ends_ready, 1)
                            act.wait_ge(delta_ready, n + 1)
                            if later(n):
                                act.wait_ge(scaled, n)
                            nc.scalar.activation(scale_to[:, :], banks[:, 6, 0:heads], ACT.Exp).then_inc(scale_ready, 1)

                        for n in range(RING):
                            stage_indices(act, n, n, stage, staged, gathered)
                        for n in range(3):
                            one_hot(n, n)
                        act.wait_ge(hot_ready, 3)
                        if many:
                            keep_hotT(0)
                            keep_hotT(1)
                            own_logit(0)
                        exponent(0, 0)
                        if many:
                            keep_hotT(2)
                        with act.Fori(0, TURNS) as i:
                            for r in range(RING):
                                j = i * RING + r
                                stage_indices(act, j + RING, r, stage, staged, gathered)
                                if many:
                                    own_logit(j + 1)
                                one_hot(j + 3, (r + 3) % RING)
                                exponent(j + 1, (r + 1) % RING)
                                if many:
                                    keep_hotT(j + 3)

                    @blk.tensor
                    def _(pe):
                        pe.sem_inc(summed_tile, RING * G)

                        def turn_hot(n, u, g):
                            if g == 0:
                                pe.wait_ge(hot_ready, n + 1)
                                if later(n, 1):
                                    pe.wait_ge(scale_ready, n - 1)
                            if later(n) or g > 0:
                                pe.wait_ge(hotT_ready, n * (G // 4) + g)
                            for q in range(4 * g, 4 * g + 4):
                                last = nc.tensor.transpose(banks[:, 6, (q % 4) * P:(q % 4 + 1) * P], hot[:, u, q, :], ident)
                            last.then_inc(hotT_psum, 1)

                        def dst_side(n):
                            blocks = load_blocks(PE_ENGINE, n)
                            if later(n):
                                pe.wait_ge(logit_ready, n)
                            for q in range(G):
                                if q % 4 == 0:
                                    pe.wait_ge(hotT_ready, n * (G // 4) + q // 4 + 1)
                                last = nc.tensor.matmul(banks[:, 7, DST_AT + q * heads:DST_AT + (q + 1) * heads], hotT[:, q, :],
                                                        scores[:, bass.ds(blocks[q], 1), :].squeeze(1), start=True, stop=True)
                            last.then_inc(dst_scores, 1)

                        def turn_val(n):
                            pe.wait_ge(val_ready, n + 1)
                            for q in range(G):
                                last = nc.tensor.transpose(banks[0:heads, q // 4, (q % 4) * P:(q % 4 + 1) * P], val[:, q * heads:(q + 1) * heads], ident)
                            last.then_inc(val_turned, 1)

                        def turn_max(n):
                            pe.wait_ge(scan_ready, ready(n))
                            pe.sem_inc(carriers, 1)
                            for q in range(G):
                                last = nc.tensor.transpose(banks[:, 7, MAX_AT + q * heads:MAX_AT + (q + 1) * heads],
                                                           maxes[:, q * P:(q + 1) * P], ident[0:heads, 0:heads])
                            last.then_inc(max_turned, 1)

                        def delta(n, u):
                            pe.wait_ge(hot_ready, n + 1)
                            pe.wait_ge(ends_ready, n + 1)
                            if later(n):
                                pe.wait_ge(scale_ready, n)
                            before, first = hot[:, (u - 1) % RING, G - 1, :], hot[:, u, 0, :]
                            nc.tensor.matmul(banks[:, 6, 0:heads], before, ends[:, u, 1, :], start=True, stop=False)
                            nc.tensor.matmul(banks[:, 6, 0:heads], first, ends[:, u, 0, :], start=False, stop=True).then_inc(delta_ready, 1)

                        def sums_of(j, u, q):
                            if many:
                                if q == 0:
                                    pe.wait_ge(weighted, j + 1)
                                by = hot[:, u, q, :]
                            else:
                                pe.wait_ge(weighted, j * G + q + 1)
                                by = weighted_hot[:, u % 2, q, :]
                            sum_tile(pe, j, q, by, rows[:, u, q, 0:sum_w], summed_tile, added, sum_w)

                        if many:
                            for n in range(2):
                                for g in range(G // 4):
                                    turn_hot(n, n, g)
                                dst_side(n)
                                if n == 0:
                                    turn_val(0)
                        else:
                            turn_val(0)
                        turn_max(0)
                        delta(0, 0)
                        turn_val(1)
                        if many:
                            for g in range(G // 4):
                                turn_hot(2, 2, g)
                        with pe.Fori(0, TURNS) as i:
                            for r in range(RING):
                                j, u, un = i * RING + r, r, (r + 1) % RING
                                for q in range(4):
                                    sums_of(j, u, q)
                                if many:
                                    dst_side(j + 2)
                                turn_max(j + 1)
                                for q in range(4, G):
                                    sums_of(j, u, q)
                                delta(j + 1, un)
                                if many:
                                    turn_hot(j + 3, (r + 3) % RING, 0)
                                turn_val(j + 2)
                                if many:
                                    turn_hot(j + 3, (r + 3) % RING, 1)

                    @blk.vector
                    def _(dve):
                        v = nc.vector
                        dve.sem_inc(scan_ready, 2)
                        dve.sem_inc(added, 4)
                        v.memset(maxes[:, :], 0.0).then_inc(scan_fwd, 1)
                        v.memset(leaky[:, :, :, :], 0.0)
                        v.memset(hot[:, RING - 1, :, :], 0.0)
                        if many:
                            v.memset(rows[:, :, :, ACC_W - 1:ACC_W], 1.0)
                        v.memset(ends[:, :, :, :], 0.0).then_inc(leaky_ready, 1)
                        dve.wait_ge(leaky_ready, 1)

                        at_dst_psum = banks[:, 7, DST_AT:DST_AT + GH]

                        def keep_dst():
                            v.tensor_copy(at_dst[:, :], at_dst_psum).then_inc(logit_ready, 1)

                        def value(n, u):
                            dve.wait_ge(gathered[u], arrived(n, u))
                            if many:
                                dve.wait_ge(dst_scores, n + 1)
                                v.tensor_tensor(val[:, :].rearrange("p (t h) -> p t h", t=G), rows[:, u, :, D:ROW0],
                                                at_dst_psum.rearrange("p (t h) -> p t h", t=G), ALU.max).then_inc(val_ready, 1)
                            else:
                                v.tensor_tensor(sums[:, 0, :].unsqueeze(2), rows[:, u, :, D + 1:D + 2], edge_q[:, bass.ds(n * G, G)].unsqueeze(2), ALU.add).then_inc(logit_ready, 1)
                                dve.wait_ge(logit_ready, n + 1)
                                v.scalar_tensor_tensor(val[:, :], sums[:, 0, :], slope, sums[:, 0, :], ALU.mult, ALU.max).then_inc(val_ready, 1)

                        def scan_on(n, w):
                            dve.wait_ge(val_turned, n + 1)
                            dve.wait_ge(restart_in[w], (n - w) * 8 + 16)
                            v.tensor_tensor_scan(maxes[:, :], restart[:, w, 0:SLOTS], scan_psum, maxes[:, SLOTS - 1:SLOTS],
                                                 ALU.add, ALU.max).then_inc(scan_fwd, 1)

                        def scan_back(n, w):
                            dve.wait_ge(scan_fwd, n + 2)
                            back = maxes[:, :][:, ::-1]
                            v.tensor_tensor_scan(back, restart[:, w, 1:SLOTS + 1][:, ::-1], back, -BIG, ALU.add, ALU.max).then_inc(scan_ready, 1)

                        top_of = banks[:, 7, MAX_AT:MAX_AT + GH]

                        def logit(n, u):
                            dve.wait_ge(logit_ready, n + 1)
                            v.tensor_tensor(sums[:, 0, :].rearrange("p (t h) -> p t h", t=G), rows[:, u, :, D:ROW0],
                                            at_dst[:, :].rearrange("p (t h) -> p t h", t=G), ALU.add)

                        def take_max(n, u):
                            dve.wait_ge(max_turned, n + 1)
                            if many:
                                v.tensor_tensor(sums[:, 2, :], top_of, at_dst[:, :], ALU.add).then_inc(sums_ready, 1)
                            else:
                                if later(n):
                                    dve.wait_ge(exp_ready, n)
                                v.tensor_tensor(power[:, 0, :], val[:, :], top_of, ALU.subtract).then_inc(power_ready, 1)
                                v.tensor_copy(leaky[:, u, 2, :], top_of).then_inc(leaky_ready, 1)

                        def leak(n, u):
                            dve.wait_ge(sums_ready, n + 1)
                            dve.wait_ge(own_ready, n + 1)
                            v.scalar_tensor_tensor(leaky[:, u, :, :], sums[:, :, :], slope, sums[:, :, :], ALU.mult, ALU.max).then_inc(leaky_ready, 1)

                        def powers(n, u):
                            dve.wait_ge(leaky_ready, n + 2)
                            if many:
                                v.tensor_tensor(power[:, :, :], leaky[:, u, 0:2, :], leaky[:, u, 2, :].unsqueeze(1).broadcast_to([P, 2, GH]),
                                                ALU.subtract).then_inc(power_ready, 1)
                                return
                            v.tensor_scalar(ends[:, u, 0, :], leaky[:, u, 2, 0:1], same_first[:, bass.ds(n, 1)], None, ALU.mult)
                            v.tensor_scalar(ends[:, u, 1, :], leaky[:, (u - 1) % RING, 2, GH - 1:GH], same_last[:, bass.ds(n, 1)], None, ALU.mult).then_inc(ends_ready, 1)

                        def weigh(n, u):
                            dve.wait_ge(exp_ready, n + 1)
                            to = rows[:, u, :, 0:D].rearrange("p t (h c) -> p t h c", h=HEADS)
                            e = rows[:, u, :, D:ROW0].unsqueeze(3).broadcast_to([P, G, HEADS, HEAD_DIM])
                            v.tensor_tensor(to, to, e, ALU.mult).then_inc(weighted, 1)

                        def rescale(j, block):
                            dve.wait_ge(scale_ready, j + 1)
                            dve.wait_ge(added, j * G + 4)
                            if many:
                                num = acc[:, bass.ds(block, 1), 0:D].squeeze(1).rearrange("p (h c) -> p h c", h=HEADS)
                                den = acc[:, bass.ds(block, 1), D:D + 2 * HEADS].squeeze(1).rearrange("p (c h) -> p c h", c=2)
                                v.tensor_tensor(num, num, scale_to[:, :].unsqueeze(2).broadcast_to([P, HEADS, HEAD_DIM]), ALU.mult)
                                v.tensor_tensor(den, den, scale_to[:, :].unsqueeze(1).broadcast_to([P, 2, HEADS]), ALU.mult).then_inc(scaled, 1)
                            else:
                                at = acc[:, bass.ds(block, 1), 0:sum_w].squeeze(1)
                                v.tensor_scalar(at, at, scale_to[:, 0:1], None, ALU.mult).then_inc(scaled, 1)
                            dve.wait_ge(scaled, j + 1)

                        value(0, 0)
                        if many:
                            keep_dst()
                        dve.wait_ge(scan_fwd, 1)
                        scan_on(0, 0)
                        scan_back(0, 0)
                        if many:
                            logit(0, 0)
                        take_max(0, 0)
                        if many:
                            leak(0, 0)
                        powers(0, 0)
                        value(1, 1)
                        if many:
                            keep_dst()
                            weigh(0, 0)
                        with dve.Fori(0, TURNS) as i:
                            for r in range(RING):
                                j, u, un, w = i * RING + r, r, (r + 1) % RING, (r + 1) % 2
                                blocks = load_blocks(DVE_ENGINE, j)

                                def add(q):
                                    add_tile(dve, j, q, blocks[q], summed_tile, added, sum_w)

                                rescale(j, blocks[0])
                                scan_on(j + 1, w)
                                add(0)
                                scan_back(j + 1, w)
                                add(1)
                                if many:
                                    logit(j + 1, un)
                                add(2)
                                take_max(j + 1, un)
                                add(3)
                                if many:
                                    leak(j + 1, un)
                                add(4)
                                powers(j + 1, un)
                                add(5)
                                value(j + 2, (r + 2) % RING)
                                add(6)
                                if many:
                                    keep_dst()
                                add(7)
                                if many:
                                    weigh(j + 1, un)

        def plain_edges(tag, table, width, filtered):
            st = ExitStack()
            with st:
                rows = sb(st, f"{tag}_rows", [P, RING, G, width])
                stage = sb(st, f"{tag}_stage", [P, RING, G], I32)
                hot = sb(st, f"{tag}_hot", [P, RING, G, P])
                if filtered:
                    scaled = sb(st, f"{tag}_scaled", [P, 2, G, RADIAL + 1])
                    edge_in = sb(st, f"{tag}_edge_in", [P, RING, G, EDGE_DIM + RADIAL])
                    scaledT = sb(st, f"{tag}_scaledT", [3 * (RADIAL + 1), 2, 3, P])
                    wr = sb(st, f"{tag}_wr", [3 * (RADIAL + 1), 3 * FILTERS])
                    we = sb(st, f"{tag}_we", [P, 2 * EDGE_DIM])
                    attn = sb(st, f"{tag}_attn", [P, 2, P])
                    we_attn = sb(st, f"{tag}_we_attn", [P, EDGE_DIM])
                    be_attn = sb(st, f"{tag}_be_attn", [P, 1])
                    logit_part = sb(st, f"{tag}_logit_part", [P, G, EDGE_DIM])
                gathered = [sem(f"{tag}_gathered{u}") for u in range(RING)]
                staged, hot_ready, summed_tile, added = (sem(f"{tag}_{n}") for n in ("staged", "hot_ready", "summed_tile", "added"))
                if filtered:
                    edge_ready = [sem(f"{tag}_edge_in{u}") for u in range(RING)]
                    (scaled_ready, turned, scaledT_ready, filters, filtered_rows, logits, products, w_in, attn_ready,
                     we_attn_psum, we_attn_ready) = (sem(f"{tag}_{n}") for n in (
                         "scaled_ready", "turned", "scaledT_ready", "filters", "filtered_rows", "logits", "products", "w_in",
                         "attn_ready", "we_attn_psum", "we_attn_ready"))
                    by_bank = ((0, 0, 3, 0), (1, 3, 6, 0), (0, 6, 7, 3), (1, 7, 8, 3))

                with nc.Block() as blk:
                    @blk.gpsimd
                    def _(pool):
                        gather_batches(pool, table, width, rows, stage, staged, gathered, summed_tile, 1)

                    if filtered:
                        @blk.sync
                        def _(sp):
                            for to, name in ((wr, "w_r2m"), (we, "we")):
                                sp.dma_start(to[:, :], inp[name]).then_inc(w_in, 16)

                            def load(n, u):
                                tiles = nc.values_load_multi_w_load_instructions(
                                    step_tile[0:1, bass.ds(n * G, G)], engines=[SP_ENGINE], min_val=0, max_val=TILES - 1,
                                    skip_runtime_bounds_check_because="clamped when they were made")[1]
                                sp.wait_ge(scaled_ready, n + 1)
                                sp.sem_inc(carriers, 1)
                                sp.wait_ge(logits, n + 1)
                                sp.sem_inc(carriers, 1)
                                for q in range(G):
                                    sp.dma_start(edge_in[:, u, q, :], inp["edge_attr"][bass.ds(tiles[q] * P, P), :]).then_inc(edge_ready[u], 16)

                            for n in range(2):
                                load(n, n)
                            with sp.Fori(0, TURNS) as i:
                                for r in range(RING):
                                    load(i * RING + r + 2, (r + 2) % RING)
                            for u in range(RING):
                                sp.wait_ge(edge_ready[u], 16 * G * (TURNS + (u < 2)))

                    @blk.scalar
                    def _(act):
                        if filtered:
                            act.sem_inc(scaledT_ready, 2)

                        def keep_scaledT(n, w):
                            act.wait_ge(turned, ready(n))
                            act.wait_ge(filters, free(n))
                            nc.scalar.copy(scaledT[:, w, :, :], banks[0:3 * (RADIAL + 1), 6 + w, 0:3 * P].rearrange("p (g e) -> p g e", g=3)).then_inc(scaledT_ready, 1)

                        for n in range(RING):
                            stage_indices(act, n, n, stage, staged, gathered)
                        if filtered:
                            keep_scaledT(0, 0)
                            keep_scaledT(1, 1)
                        with act.Fori(0, TURNS) as i:
                            for r in range(RING):
                                stage_indices(act, i * RING + r + RING, r, stage, staged, gathered)
                                if filtered:
                                    keep_scaledT(i * RING + r + 2, r % 2)

                    @blk.tensor
                    def _(pe):
                        pe.sem_inc(summed_tile, RING * G)
                        if filtered:
                            pe.sem_inc(turned, 2)
                            pe.sem_inc(filters, 2)
                            pe.wait_ge(w_in, 32)
                            pe.wait_ge(attn_ready, 1)
                            for c0, c1, rhs in ((0, EDGE_DIM, lambda k: we[:, k * EDGE_DIM:(k + 1) * EDGE_DIM]), (EDGE_DIM, EDGE_DIM + 1, lambda k: col("be", k))):
                                for k in range(2):
                                    last = nc.tensor.matmul(banks[:, 2, c0:c1], attn[:, k, :], rhs(k), start=(k == 0), stop=(k == 1))
                            last.then_inc(we_attn_psum, 1)
                            pe.wait_ge(we_attn_ready, 1)

                        def turn_scaled(n, w):
                            pe.wait_ge(scaled_ready, n + RING + 1)
                            pe.wait_ge(scaledT_ready, free(n))
                            for g, q in enumerate((0, 3, 5)):
                                last = nc.tensor.transpose(banks[0:3 * (RADIAL + 1), 6 + w, g * P:(g + 1) * P],
                                                           scaled[:, w, q:q + 3, :].rearrange("p q c -> p (q c)"), ident)
                            last.then_inc(turned, 1)

                        def make_filters(n, w):
                            pe.wait_ge(scaledT_ready, ready(n))
                            if later(n):
                                pe.wait_ge(filtered_rows, n)
                            for bank, q0, q1, at in by_bank:
                                g, c = min(q0 // 3, 2), (q0 - (0, 3, 5)[min(q0 // 3, 2)])
                                last = nc.tensor.matmul(banks[:, bank, at * P:(at + q1 - q0) * P], scaledT[:, w, g, :],
                                                        wr[:, c * FILTERS:(c + q1 - q0) * FILTERS], start=True, stop=True)
                            last.then_inc(filters, 1)

                        def sums_of(j, u, q):
                            if q == 0:
                                if filtered:
                                    pe.wait_ge(filtered_rows, j + 1)
                                else:
                                    pe.wait_ge(gathered[u], arrived(j, u))
                                pe.wait_ge(hot_ready, j + 1)
                            sum_tile(pe, j, q, hot[:, u, q, :], rows[:, u, q, :], summed_tile, added, width)

                        if filtered:
                            turn_scaled(0, 0)
                            turn_scaled(1, 1)
                            make_filters(0, 0)
                        with pe.Fori(0, TURNS) as i:
                            for r in range(RING):
                                j, u = i * RING + r, r
                                for q in range(G // 2):
                                    sums_of(j, u, q)
                                if filtered:
                                    make_filters(j + 1, (r + 1) % 2)
                                for q in range(G // 2, G):
                                    sums_of(j, u, q)
                                if filtered:
                                    turn_scaled(j + 2, r % 2)

                    @blk.vector
                    def _(dve):
                        v = nc.vector
                        dve.sem_inc(added, 4)
                        if filtered:
                            dve.sem_inc(logits, RING)
                            dve.sem_inc(scaled_ready, RING)
                            for k in range(2):
                                last = v.tensor_scalar(attn[:, k, :], ones[:, :], col("attn", k), None, ALU.mult)
                            last.then_inc(attn_ready, 1)
                            dve.wait_ge(we_attn_psum, 1)
                            v.tensor_copy(we_attn[:, :], banks[:, 2, 0:EDGE_DIM])
                            v.tensor_copy(be_attn[:, :], banks[:, 2, EDGE_DIM:EDGE_DIM + 1]).then_inc(we_attn_ready, 1)
                            dve.wait_ge(we_attn_ready, 1)

                        def one_hot(n, u):
                            where = dst_loc[:, bass.ds(n * G, G)]
                            v.tensor_tensor(hot[:, u, :, :], iota_n.unsqueeze(1).broadcast_to([P, G, P]),
                                            where.unsqueeze(2).broadcast_to([P, G, P]), ALU.is_equal).then_inc(hot_ready, 1)

                        def scale_radial(n, u, w):
                            dve.wait_ge(edge_ready[u], arrived(n, u))
                            dve.wait_ge(turned, free(n))
                            by = cutoff[:, bass.ds(n * G, G)].unsqueeze(2)
                            v.tensor_copy(scaled[:, w, :, RADIAL:], by)
                            v.tensor_tensor(scaled[:, w, :, 0:RADIAL], edge_in[:, u, :, EDGE_DIM:], by.broadcast_to([P, G, RADIAL]), ALU.mult).then_inc(scaled_ready, 1)

                        def filter_rows(n, u, part):
                            if part == 0:
                                dve.wait_ge(gathered[u], arrived(n, u))
                                dve.wait_ge(filters, ready(n))
                            for bank, q0, q1, at in by_bank[2 * part:2 * part + 2]:
                                to = rows[:, u, q0:q1, :]
                                last = v.tensor_tensor(to, to, banks[:, bank, at * P:(at + q1 - q0) * P].rearrange("p (q f) -> p q f", q=q1 - q0), ALU.mult)
                            if part == 1:
                                last.then_inc(filtered_rows, 1)

                        def logit_products(n, u):
                            dve.wait_ge(edge_ready[u], arrived(n, u))
                            dve.wait_ge(logits, n + RING)
                            v.tensor_tensor(logit_part[:, :, :], edge_in[:, u, :, 0:EDGE_DIM], we_attn[:, :].unsqueeze(1).broadcast_to([P, G, EDGE_DIM]), ALU.mult).then_inc(products, 1)

                        def edge_logits(n):
                            dve.wait_ge(products, n + 1)
                            v.tensor_reduce(edge_q[:, bass.ds(n * G, G)], logit_part[:, :, :], AX_X, ALU.add).then_inc(logits, 1)

                        one_hot(0, 0)
                        if filtered:
                            for n in range(2):
                                scale_radial(n, n, n)
                                logit_products(n, n)
                                edge_logits(n)
                            for part in range(2):
                                filter_rows(0, 0, part)
                        with dve.Fori(0, TURNS) as i:
                            for r in range(RING):
                                j, u, un, u2 = i * RING + r, r, (r + 1) % RING, (r + 2) % RING
                                blocks = load_blocks(DVE_ENGINE, j)

                                def add(q):
                                    add_tile(dve, j, q, blocks[q], summed_tile, added, width)

                                if filtered:
                                    logit_products(j + 2, u2)
                                add(0)
                                if filtered:
                                    edge_logits(j + 2)
                                add(1)
                                one_hot(j + 1, un)
                                add(2)
                                if filtered:
                                    filter_rows(j + 1, un, 0)
                                add(3)
                                if filtered:
                                    filter_rows(j + 1, un, 1)
                                add(4)
                                if filtered:
                                    scale_radial(j + 2, u2, r % 2)
                                for q in range(5, G):
                                    add(q)
                        if filtered:
                            dve.wait_ge(logits, BATCHES + 2 + RING)
                            v.tensor_scalar(edge_q[:, 0:(BATCHES + 2) * G], edge_q[:, 0:(BATCHES + 2) * G], be_attn[:, 0:1], None, ALU.add)

        def column_stats(dve, RT, part, i, width, last, done):
            dve.wait_ge(done, ready(i))
            for f in range(2):
                nc.vector.bn_stats(part[:, f, bass.ds(i, 1), :].squeeze(1), RT[:, f, bass.ds(i * width, last if isinstance(i, int) else width)])

        def column_norm(dve, part, count, whole, scaling, gamma, beta, steps, root_ready):
            v = nc.vector
            n = 0

            def link(ins):
                nonlocal n
                n += 1
                ins.then_inc(steps, 1)
                dve.wait_ge(steps, n)

            link(v.memset(scaling[:, :, :], 0.0))
            for f in range(2):
                last = v.bn_aggr(whole[:, f, :], part[:, f, 0:count, :].rearrange("p i s -> p (i s)"))
            link(last)
            dve.wait_ge(root_ready, 1)
            link(v.reciprocal(whole[:, :, 1], scaling[:, 0, :]))
            link(v.tensor_tensor(scaling[:, 0, :], whole[:, :, 1], cols[:, COLS[gamma][0]:COLS[gamma][1]], ALU.mult))
            link(v.tensor_tensor(whole[:, :, 0], whole[:, :, 0], scaling[:, 0, :], ALU.mult))
            link(v.tensor_tensor(scaling[:, 1, :], cols[:, COLS[beta][0]:COLS[beta][1]], whole[:, :, 0], ALU.subtract))

        BN_VAR_STEP = 2

        def column_root(act, whole, scaling, steps, root_ready):
            act.wait_ge(steps, BN_VAR_STEP)
            nc.scalar.activation(scaling[:, 0, :], whole[:, :, 1], ACT.Sqrt, bias=eps[:, 0:1]).then_inc(root_ready, 1)

        def layer0_tail():
            st = ExitStack()
            with st:
                RT = sb(st, "RT", [P, 2, N_PAD])
                part = sb(st, "bn_part", [P, 2, NB, 6])
                whole = sb(st, "bn_whole", [P, 2, 2])
                scaling = [sb(st, f"bn_scaling{i}", [P, 2, 2]) for i in range(2)]
                attention_out(RT, part, whole, scaling[0])
                feed_forward(RT, part, whole, scaling)
                add_layer0(RT, scaling[1])

        def attention_out(RT, part, whole, scaling):
            st = ExitStack()
            with st:
                wo = sb(st, "wo", [P, 2 * D])
                values = sb(st, "values", [P, 2, D])
                own = sb(st, "own", [P, NB, HEADS])
                share = sb(st, "share", [P, NB, HEADS])
                per_node = sb(st, "per_node", [P, 3, NB])
                att = sb(st, "att", [P, 2, D])
                att_sum = sb(st, "att_sum", [P, 2, D])
                h = sb(st, "ao_h", [P, 2, D])
                attT = sb(st, "attT", [P, 2, 2, P])
                w_in, steps, root = sem("ao_w_in"), sem("ao_steps"), sem("ao_root")
                values_in = [sem(f"ao_values_in{u}") for u in range(2)]
                own_part, with_sum, att_ready, turned, attT_ready, h_ready, product, kept = (sem(f"ao_{n}") for n in (
                    "own_part", "with_sum", "att_ready", "turned", "attT_ready", "h_ready", "product", "kept"))
                bn_steps, bn_root = sem("ao_bn_steps"), sem("ao_bn_root")
                DEG_STEP = 2

                with nc.Block() as blk:
                    @blk.sync
                    def _(sp):
                        sp.dma_start(wo[:, :], inp["wo"]).then_inc(w_in, 16)

                        def load(b, u, _):
                            sp.wait_ge(own_part, free(b))
                            sp.sem_inc(carriers, 1)
                            sp.dma_start(values[:, u, :], node_rows(table0, b)[:, 0:D]).then_inc(values_in[u], 16)

                        each_pair(sp, NB, load)

                    @blk.scalar
                    def _(act):
                        act.sem_inc(attT_ready, 2)
                        act.sem_inc(h_ready, 2)
                        act.sem_inc(kept, 2)
                        act.wait_ge(steps, DEG_STEP)
                        nc.scalar.activation(per_node[:, 2, :], degree[:, :], ACT.Sqrt, bias=ones[:, 0:1]).then_inc(root, 1)

                        def prepare(b, u):
                            act.wait_ge(product, free(b))
                            nc.scalar.activation(h[:, u, :], X[:, bass.ds(b, 1), :].squeeze(1), ACT.Relu,
                                                 bias=nbias[:, bass.ds(b, 1)], scale=rstd[:, bass.ds(b, 1)]).then_inc(h_ready, 1)
                            act.wait_ge(turned, ready(b))
                            nc.scalar.copy(attT[:, u, :, :], banks[:, u, 0:D].rearrange("p (f n) -> p f n", f=2)).then_inc(attT_ready, 1)

                        def block(b, u, more):
                            if more:
                                prepare(b + 1, 1 - u)
                            act.wait_ge(product, ready(b))
                            for f in range(2):
                                last = nc.scalar.activation(RT[:, f, bass.ds(b * P, P)], banks[:, 2 + u, f * P:(f + 1) * P], ACT.Identity, bias=col("bo", f))
                            last.then_inc(kept, 1)

                        prepare(0, 0)
                        each_pair(act, NB, block)
                        column_root(act, whole, scaling, bn_steps, bn_root)

                    @blk.tensor
                    def _(pe):
                        pe.sem_inc(turned, 2)
                        pe.sem_inc(product, 2)
                        pe.wait_ge(w_in, 16)

                        def turn(b, u):
                            pe.wait_ge(att_ready, ready(b))
                            pe.wait_ge(attT_ready, free(b))
                            for f in range(2):
                                last = nc.tensor.transpose(banks[:, u, f * P:(f + 1) * P], att[:, u, f * P:(f + 1) * P], ident)
                            last.then_inc(turned, 1)

                        def block(b, u, more):
                            if more:
                                turn(b + 1, 1 - u)
                            pe.wait_ge(attT_ready, ready(b))
                            pe.wait_ge(h_ready, ready(b))
                            pe.wait_ge(kept, free(b))
                            for f in range(2):
                                to = banks[:, 2 + u, f * P:(f + 1) * P]
                                for k in range(2):
                                    nc.tensor.matmul(to, wo[:, k * D + f * P:k * D + (f + 1) * P], attT[:, u, k, :], start=(k == 0), stop=False)
                                last = nc.tensor.matmul(to, h[:, u, f * P:(f + 1) * P], ident, start=False, stop=True)
                            last.then_inc(product, 1)

                        turn(0, 0)
                        each_pair(pe, NB, block)

                    @blk.vector
                    def _(dve):
                        v = nc.vector
                        dve.sem_inc(own_part, 2)
                        dve.sem_inc(att_ready, 2)
                        n = 0

                        def link(ins):
                            nonlocal n
                            n += 1
                            ins.then_inc(steps, 1)
                            dve.wait_ge(steps, n)

                        v.tensor_copy(degree[:, :], acc[:, :, ACC_W - 1])
                        link(v.tensor_scalar(per_node[:, 0, :], acc[:, :, ACC_W - 1], 1.0, None, ALU.max))
                        v.tensor_scalar(per_node[:, 1, :], degree[:, :], 0.0, None, ALU.is_equal)
                        link(v.reciprocal(per_node[:, 0, :], per_node[:, 0, :]))
                        link(v.tensor_tensor(own[:, :, :], acc[:, :, D + HEADS:D + 2 * HEADS], per_node[:, 0, :].unsqueeze(2).broadcast_to([P, NB, HEADS]), ALU.mult))
                        link(v.tensor_tensor(own[:, :, :], own[:, :, :], per_node[:, 1, :].unsqueeze(2).broadcast_to([P, NB, HEADS]), ALU.add))
                        link(v.tensor_tensor(share[:, :, :], acc[:, :, D:ROW0], own[:, :, :], ALU.add))
                        dve.wait_ge(root, 1)
                        v.reciprocal(dinv[:, :], per_node[:, 2, :])
                        link(v.reciprocal(share[:, :, :], share[:, :, :]))

                        def by_head(ap, b):
                            return ap[:, bass.ds(b, 1), :].squeeze(1).unsqueeze(2).broadcast_to([P, HEADS, HEAD_DIM])

                        def split(ap):
                            return ap.rearrange("p (h c) -> p h c", h=HEADS)

                        def own_share(b, u):
                            dve.wait_ge(values_in[u], (b - u) * 8 + 16)
                            if later(b, 1):
                                dve.wait_ge(att_ready, free(b))
                            v.tensor_tensor(split(att_sum[:, u, :]), split(values[:, u, :]), by_head(own, b), ALU.mult).then_inc(own_part, 1)

                        def block(b, u, more):
                            dve.wait_ge(own_part, ready(b))
                            v.tensor_tensor(att_sum[:, u, :], att_sum[:, u, :], acc[:, bass.ds(b, 1), 0:D].squeeze(1), ALU.add).then_inc(with_sum, 1)
                            if more:
                                own_share(b + 1, 1 - u)
                            dve.wait_ge(with_sum, b + 1)
                            dve.wait_ge(turned, free(b))
                            v.tensor_tensor(split(att[:, u, :]), split(att_sum[:, u, :]), by_head(share, b), ALU.mult).then_inc(att_ready, 1)
                            if later(b, 3):
                                column_stats(dve, RT, part, b - 4, P, P, kept)

                        own_share(0, 0)
                        each_pair(dve, NB, block, 4)
                        for b in range(NB - 4, NB):
                            column_stats(dve, RT, part, b, P, min(P, N_NODES - b * P), kept)
                        column_norm(dve, part, NB, whole, scaling, "bn1_g", "bn1_b", bn_steps, bn_root)

        def feed_forward(RT, part, whole, scaling):
            st = ExitStack()
            with st:
                w1 = sb(st, "w1", [P, 2 * FF])
                w2 = sb(st, "w2", [P, 4 * D])
                hidden = sb(st, "hidden", [P, 2, 4, CHUNK])
                w_in = sem("ff_w_in")
                normed, up, hidden_ready, down, merged = (sem(f"ff_{n}") for n in ("normed", "up", "hidden_ready", "down", "merged"))
                bn_steps, bn_root = sem("ff_bn_steps"), sem("ff_bn_root")
                M = FF // P

                with nc.Block() as blk:
                    @blk.sync
                    def _(sp):
                        sp.dma_start(w1[:, :], inp["w1"]).then_inc(w_in, 16)
                        sp.dma_start(w2[:, :], inp["w2"]).then_inc(w_in, 16)

                    @blk.scalar
                    def _(act):
                        act.sem_inc(hidden_ready, M)

                        def norm(c):
                            for f in range(2):
                                at = RT[:, f, bass.ds(c * CHUNK, CHUNK)]
                                last = nc.scalar.activation(at, at, ACT.Identity, bias=scaling[0][:, 1, f:f + 1], scale=scaling[0][:, 0, f:f + 1])
                            last.then_inc(normed, 1)

                        def chunk(c, u, more):
                            if more:
                                norm(c + 1)
                            for m in range(M):
                                act.wait_ge(up, c * M + m + 1)
                                act.wait_ge(down, free(c))
                                nc.scalar.activation(hidden[:, u, m, :], banks[:, m, 0:CHUNK], ACT.Relu, bias=col("b1", m)).then_inc(hidden_ready, 1)

                        norm(0)
                        each_pair(act, CHUNKS, chunk)
                        column_root(act, whole, scaling[1], bn_steps, bn_root)

                    @blk.tensor
                    def _(pe):
                        pe.sem_inc(down, 2)
                        pe.wait_ge(w_in, 32)

                        def go_up(c):
                            pe.wait_ge(normed, c + 1)
                            for m in range(M):
                                pe.wait_ge(hidden_ready, c * M + m + 1)
                                for k in range(2):
                                    last = nc.tensor.matmul(banks[:, m, 0:CHUNK], w1[:, k * FF + m * P:k * FF + (m + 1) * P],
                                                            RT[:, k, bass.ds(c * CHUNK, CHUNK)], start=(k == 0), stop=(k == 1))
                                last.then_inc(up, 1)

                        def chunk(c, u, more):
                            if more:
                                go_up(c + 1)
                            pe.wait_ge(hidden_ready, (c + 1) * M + M)
                            pe.wait_ge(merged, free(c))
                            for f in range(2):
                                for m in range(M):
                                    last = nc.tensor.matmul(banks[:, 4 + 2 * u + f, 0:CHUNK], w2[:, m * D + f * P:m * D + (f + 1) * P],
                                                            hidden[:, u, m, :], start=(m == 0), stop=(m == M - 1))
                            last.then_inc(down, 1)

                        go_up(0)
                        each_pair(pe, CHUNKS, chunk)

                    @blk.vector
                    def _(dve):
                        v = nc.vector
                        dve.sem_inc(merged, 2)

                        def chunk(c, u, _):
                            dve.wait_ge(down, ready(c))
                            for f in range(2):
                                at = RT[:, f, bass.ds(c * CHUNK, CHUNK)]
                                last = v.scalar_tensor_tensor(at, banks[:, 4 + 2 * u + f, 0:CHUNK], col("b2", f), at, ALU.add, ALU.add)
                            last.then_inc(merged, 1)
                            if later(c):
                                column_stats(dve, RT, part, c - 1, CHUNK, CHUNK, merged)

                        each_pair(dve, CHUNKS, chunk, 2)
                        column_stats(dve, RT, part, CHUNKS - 1, CHUNK, N_NODES - (CHUNKS - 1) * CHUNK, merged)
                        column_norm(dve, part, CHUNKS, whole, scaling[1], "bn2_g", "bn2_b", bn_steps, bn_root)

        def add_layer0(RT, scaling):
            st = ExitStack()
            with st:
                normed = sb(st, "al_normed", [P, 2, 2, P])
                normed_ready, turned, updated = sem("al_normed_ready"), sem("al_turned"), sem("al_updated")
                with nc.Block() as blk:
                    @blk.scalar
                    def _(act):
                        act.sem_inc(normed_ready, 2)

                        def block(b, u, _):
                            act.wait_ge(turned, free(b))
                            for f in range(2):
                                last = nc.scalar.activation(normed[:, u, f, :], RT[:, f, bass.ds(b * P, P)], ACT.Identity,
                                                            bias=scaling[:, 1, f:f + 1], scale=scaling[:, 0, f:f + 1])
                            last.then_inc(normed_ready, 1)

                        each_pair(act, NB, block)

                    @blk.tensor
                    def _(pe):
                        pe.sem_inc(turned, 2)

                        def block(b, u, _):
                            pe.wait_ge(normed_ready, ready(b))
                            pe.wait_ge(updated, free(b))
                            for f in range(2):
                                last = nc.tensor.transpose(banks[:, u, f * P:(f + 1) * P], normed[:, u, f, :], ident)
                            last.then_inc(turned, 1)

                        each_pair(pe, NB, block)

                    @blk.vector
                    def _(dve):
                        dve.sem_inc(updated, 2)

                        def block(b, u, _):
                            dve.wait_ge(turned, ready(b))
                            add_to_x(dve, b, banks[:, u, 0:D], updated)

                        each_pair(dve, NB, block, 2)
                        row_stats(dve, NB - 1, updated)

        def add_to_x(dve, b, what, updated):
            at = X[:, bass.ds(b, 1), :].squeeze(1)
            nc.vector.tensor_tensor(at, at, what, ALU.add).then_inc(updated, 1)
            if later(b):
                row_stats(dve, b - 1, updated)

        def row_stats(dve, b, updated):
            dve.wait_ge(updated, ready(b))
            nc.vector.bn_stats(stats[:, bass.ds(b, 1), :].squeeze(1), X[:, bass.ds(b, 1), :].squeeze(1))

        def filter_out():
            st = ExitStack()
            with st:
                w = sb(st, "fo_w", [P, FILTERS + D])
                agg = sb(st, "fo_agg", [P, 2, FILTERS])
                aggT = sb(st, "fo_aggT", [P, 2, P])
                lin = sb(st, "fo_lin", [P, 2, P])
                w_in = sem("fo_w_in")
                agg_ready, turned, aggT_ready, lin_psum, lin_ready, product, updated = (sem(f"fo_{n}") for n in (
                    "agg_ready", "turned", "aggT_ready", "lin_psum", "lin_ready", "product", "updated"))
                with nc.Block() as blk:
                    @blk.sync
                    def _(sp):
                        sp.dma_start(w[:, :], inp["w_out1"]).then_inc(w_in, 16)

                    @blk.scalar
                    def _(act):
                        for s_ in (agg_ready, aggT_ready, lin_ready):
                            act.sem_inc(s_, 2)

                        def take(b, u):
                            act.wait_ge(turned, free(b))
                            nc.scalar.copy(agg[:, u, :], acc[:, bass.ds(b, 1), 0:FILTERS].squeeze(1)).then_inc(agg_ready, 1)

                        def add_bias(b, u):
                            act.wait_ge(lin_psum, ready(b))
                            act.wait_ge(product, free(b))
                            nc.scalar.activation(lin[:, u, :], banks[:, 2 + u, 0:P], ACT.Identity, bias=col("b_lin2")).then_inc(lin_ready, 1)

                        def block(b, u, more):
                            if more:
                                take(b + 1, 1 - u)
                            act.wait_ge(turned, ready(b))
                            act.wait_ge(lin_psum, free(b))
                            nc.scalar.copy(aggT[:, u, :], banks[:, u, 0:P]).then_inc(aggT_ready, 1)
                            if later(b):
                                add_bias(b - 1, 1 - u)

                        take(0, 0)
                        each_pair(act, NB, block, 2)
                        add_bias(NB - 1, (NB - 1) % 2)

                    @blk.tensor
                    def _(pe):
                        for s_ in (turned, lin_psum, product):
                            pe.sem_inc(s_, 2)
                        pe.wait_ge(w_in, 16)

                        def turn(b, u):
                            pe.wait_ge(agg_ready, ready(b))
                            pe.wait_ge(aggT_ready, free(b))
                            nc.tensor.transpose(banks[:, u, 0:P], agg[:, u, :], ident).then_inc(turned, 1)

                        def block(b, u, more):
                            if more:
                                turn(b + 1, 1 - u)
                            pe.wait_ge(aggT_ready, ready(b))
                            pe.wait_ge(lin_ready, free(b))
                            nc.tensor.matmul(banks[:, 2 + u, 0:P], w[:, 0:FILTERS], aggT[:, u, :], start=True, stop=True).then_inc(lin_psum, 1)
                            if later(b):
                                to_node(b - 1, 1 - u)

                        def to_node(b, u):
                            pe.wait_ge(lin_ready, ready(b))
                            pe.wait_ge(updated, free(b))
                            nc.tensor.matmul(banks[:, 4 + u, 0:D], lin[:, u, :], w[:, FILTERS:FILTERS + D], start=True, stop=True).then_inc(product, 1)

                        turn(0, 0)
                        each_pair(pe, NB, block, 2)
                        to_node(NB - 1, (NB - 1) % 2)

                    @blk.vector
                    def _(dve):
                        dve.sem_inc(updated, 2)

                        def block(b, u, _):
                            dve.wait_ge(product, ready(b))
                            add_to_x(dve, b, banks[:, 4 + u, 0:D], updated)

                        each_pair(dve, NB, block, 2)
                        row_stats(dve, NB - 1, updated)

        def gat_out():
            st = ExitStack()
            with st:
                share = sb(st, "go_share", [P, NB])
                part = sb(st, "go_part", [P, 2, D])
                steps, part_ready, updated = sem("go_steps"), sem("go_part_ready"), sem("go_updated")
                with nc.Block() as blk:
                    @blk.vector
                    def _(dve):
                        v = nc.vector
                        dve.sem_inc(updated, 2)
                        v.tensor_scalar(share[:, :], acc[:, :, D], 1e-16, None, ALU.add).then_inc(steps, 1)
                        dve.wait_ge(steps, 1)
                        v.reciprocal(share[:, :], share[:, :]).then_inc(steps, 1)
                        dve.wait_ge(steps, 2)

                        def relu(b, u):
                            dve.wait_ge(updated, free(b))
                            v.tensor_scalar(part[:, u, :], acc[:, bass.ds(b, 1), 0:D].squeeze(1), share[:, bass.ds(b, 1)], 0.0,
                                            ALU.mult, ALU.max).then_inc(part_ready, 1)

                        def block(b, u, more):
                            if more:
                                relu(b + 1, 1 - u)
                            dve.wait_ge(part_ready, b + 1)
                            add_to_x(dve, b, part[:, u, :], updated)

                        relu(0, 0)
                        each_pair(dve, NB, block, 2)
                        row_stats(dve, NB - 1, updated)

        def gcn_out():
            st = ExitStack()
            with st:
                part = sb(st, "gc_part", [P, 2, D])
                part_ready, updated, out_done = (sem(f"gc_{n}") for n in ("part_ready", "updated", "out_done"))
                OUT = 4
                with nc.Block() as blk:
                    @blk.sync
                    def _(sp):
                        with sp.Fori(0, (NB - 1) // OUT) as i:
                            sp.wait_ge(updated, ready(OUT * i + OUT - 1))
                            sp.sem_inc(carriers, 1)
                            sp.dma_start(out[bass.ds(i * OUT * P, OUT * P), :].rearrange("(b p) d -> p b d", p=P),
                                         X[:, bass.ds(i * OUT, OUT), :]).then_inc(out_done, 16)
                        sp.wait_ge(updated, ready(NB - 1))
                        sp.dma_start(out[(NB - 1) * P:N_NODES, :], X[0:LAST, NB - 1, :]).then_inc(out_done, 16)
                        sp.wait_ge(out_done, 16 * ((NB - 1) // OUT + 1))

                    @blk.vector
                    def _(dve):
                        v = nc.vector
                        dve.sem_inc(updated, 2)

                        def scale(b, u):
                            dve.wait_ge(updated, free(b))
                            v.scalar_tensor_tensor(part[:, u, :], acc[:, bass.ds(b, 1), 0:D].squeeze(1), dinv[:, bass.ds(b, 1)], gcn_bias[:, :],
                                                   ALU.mult, ALU.add).then_inc(part_ready, 1)

                        def block(b, u, more):
                            if more:
                                scale(b + 1, 1 - u)
                            dve.wait_ge(part_ready, b + 1)
                            at = X[:, bass.ds(b, 1), :].squeeze(1)
                            v.scalar_tensor_tensor(at, part[:, u, :], 0.0, at, ALU.max, ALU.add).then_inc(updated, 1)

                        scale(0, 0)
                        each(4, dve, NB, lambda b, u, more: block(b, u % 2, more))

        node_stage("n0", inp["wqkv"], 6 * D, qkv_load, qkv_mm, None, qkv_row, None, keep_scores, table0, ROW0, (), qkv_alloc)
        softmax_edges("e0", table0, ROW0, ACC_W, HEADS)
        layer0_tail()
        layer_ends()

        node_stage("n1", inp["w_n2m"], 3 * FILTERS, None, filter_mm, filter_mm2, filter_row, filter_mid, None, table1, FILTERS, (), filter_alloc)
        plain_edges("e1", table1, FILTERS, True)
        filter_out()
        layer_ends()

        node_stage("n2", inp["wn"], 2 * D, wn_load, wn_mm, None, wn_row, None, None, table2, ROW2, ((D, 1.0),), wn_alloc)
        softmax_edges("e2", table2, ROW2, D + 1, 1)
        gat_out()
        layer_ends()

        node_stage("n3", inp["w3"], 2 * D, None, gcn_mm, None, gcn_row, None, keep_own, table3, D, (), None)
        plain_edges("e3", table3, D, False)
        gcn_out()


def constants():
    c = np.zeros((P, CONST_W), np.float32)
    p = np.arange(P)

    def part(name):
        return c[:, CONST[name][0]:CONST[name][1]]

    part("iota_k")[:] = np.arange(STEPS)
    part("iota_n")[:] = p
    part("ident")[:] = np.eye(P)
    part("tile")[:] = np.arange(GROUPS) * P + p[:, None]
    part("p_first")[0] = -1
    part("p_last")[P - 1] = 1
    return c


def kernel(**inputs):
    import concourse.bacc as bacc
    from concourse.bass_utils import run_bass_kernel_spmd

    def a(name):
        return np.asarray(inputs[name])

    def padded(array, rows, value=0):
        fill = np.full((rows - array.shape[0],) + array.shape[1:], value, array.dtype)
        return np.ascontiguousarray(np.concatenate([array, fill]))

    def chunks(w):
        return np.ascontiguousarray(np.concatenate([w[k:k + P] for k in range(0, w.shape[0], P)], axis=1))

    def by_partition(name):
        return a(name).reshape(-1, P).T

    g, l1, l2 = "L0_gnn_", "L1_gnn_", "L2_gnn_"
    w_r2m = np.zeros((3 * (RADIAL + 1), 3 * FILTERS), np.float32)
    for q in range(3):
        to = w_r2m[q * (RADIAL + 1):(q + 1) * (RADIAL + 1), q * FILTERS:(q + 1) * FILTERS]
        to[0:RADIAL] = a(l1 + "W_r2m").T
        to[RADIAL] = a(l1 + "b_r2m")
    arrays = {
        "const": constants(),
        "x": padded(a("x"), N_PAD),
        "src": padded(a("src"), E_PAD),
        "dst": padded(a("dst"), E_PAD + P, NO_NODE),
        "edge_weight": padded(a("edge_weight"), E_PAD),
        "edge_attr": padded(np.concatenate([a("edge_attr_128"), a("edge_attr_32")], axis=1), TILES * P),
        "cols": np.ascontiguousarray(np.concatenate([by_partition(n) for n in (
            g + "bo", g + "bn1_g", g + "bn1_b", g + "b1", g + "b2", g + "bn2_g", g + "bn2_b",
            l1 + "b_n2m", l1 + "b_lin2", l2 + "be", l2 + "attn")], axis=1)),
        "wqkv": chunks(np.concatenate([a(g + "Wq"), a(g + "Wk"), a(g + "Wv")], axis=1)),
        "bqkv": np.concatenate([a(g + "bq"), a(g + "bk"), a(g + "bv")]),
        "wo": chunks(a(g + "Wo")),
        "w1": chunks(a(g + "W1")),
        "w2": chunks(a(g + "W2")),
        "w_n2m": np.ascontiguousarray(np.concatenate([chunks(a(l1 + "W_n2m").T), a(l1 + "W_lin1").T], axis=1)),
        "w_r2m": w_r2m,
        "w_out1": np.ascontiguousarray(np.concatenate([a(l1 + "W_lin2").T, a(l1 + "W_m2n").T], axis=1)),
        "wn": chunks(a(l2 + "Wn").T),
        "bn_attn": np.concatenate([a(l2 + "bn"), a(l2 + "attn").reshape(-1)]),
        "we": chunks(a(l2 + "We")),
        "w3": chunks(a("L3_gnn_W")),
        "b3": a("L3_gnn_b"),
    }
    nc = bacc.Bacc("TRN2", target_bir_lowering=False, num_devices=1)
    inp = {n: nc.dram_tensor(f"in_{n}", v.shape, mybir.dt.from_np(v.dtype), kind="ExternalInput").ap() for n, v in arrays.items()}
    out = nc.dram_tensor("out", (N_NODES, D), F32, kind="ExternalOutput").ap()
    build(nc, inp, out)
    r = run_bass_kernel_spmd(nc, [{f"in_{n}": v for n, v in arrays.items()}], core_ids=[0])
    return r.results[0]["out"]
```
